# Optimizing a Trainium2 kernel written in Bass

```python
import numpy as np
import jax
import jax.numpy as jnp

def _softmax(x, axis=-1):
    return jax.nn.softmax(x, axis=axis)

def _gelu(x):
    return jax.nn.gelu(x, approximate=True)

def _silu(x):
    return jax.nn.silu(x)

def _sigmoid(x):
    return jax.nn.sigmoid(x)

def _layernorm(x, axis=-1, eps=1e-05):
    m = jnp.mean(x, axis=axis, keepdims=True)
    v = jnp.var(x, axis=axis, keepdims=True)
    return (x - m) / jnp.sqrt(v + eps)

def _scatter_add(tgt, idx, src, axis=0):
    return tgt.at[idx].add(src)

def _segment_sum(src, seg, n):
    return jax.ops.segment_sum(src, seg, n)
kernel_name = 'mk_xattn_ffn_d4_seqx_r4_bdf54a'

def setup_inputs(seed: int=0):
    np.random.seed(seed)
    _w = jnp.asarray

    def _rec_inputs():
        import jax
        import jax.numpy as jnp
        _rk = jax.random.key(seed)
        x = 0.0002417 + 0.9998 * jax.random.normal(jax.random.fold_in(_rk, 1), (8, 512, 256), jnp.float32)
        _lenS = 512 - jax.random.randint(jax.random.fold_in(_rk, 7), (8,), 0, max(1, 512 // 4) + 1, jnp.int32)
        _lenS2 = 512 - jax.random.randint(jax.random.fold_in(_rk, 8), (8,), 0, max(1, 512 // 4) + 1, jnp.int32)
        _ctx_1024P = jax.random.normal(jax.random.fold_in(_rk, 11), (8, 16, 256), jnp.float32)
        _ctx_1024c = jax.random.dirichlet(jax.random.fold_in(_rk, 511), 0.3 * jnp.ones((16,), jnp.float32), (8, 512))
        _ctx_1024t = jnp.einsum('bsk,bkd->bsd', _ctx_1024c, _ctx_1024P)
        _ctx_1024t = _ctx_1024t * jax.lax.rsqrt(jnp.mean(jnp.square(_ctx_1024t)) + 1e-12) * 0.953939
        ctx_1024 = 7.22013e-05 + 1.00017 * (_ctx_1024t + 0.3 * jax.random.normal(jax.random.fold_in(_rk, 611), (8, 512, 256), jnp.float32))
        _validS = jnp.arange(512)[None, :] < _lenS[:, None]
        _validS2 = jnp.arange(512)[None, :] < _lenS2[:, None]
        _causal = jnp.tril(jnp.ones((512, 512), dtype=bool))
        mask_Bx1xSxS2_ik1 = jnp.where(jnp.broadcast_to(_validS2[:, None, None, :], (8, 1, 512, 512)), 1, 0).astype(jnp.int32)
        mask_Bx1x1xS2_ff0 = jnp.where(jnp.ones((8, 1, 1, 512), dtype=bool), 0.0, -1000000000.0).astype(jnp.float32)
        return (x, ctx_1024, mask_Bx1xSxS2_ik1, mask_Bx1x1xS2_ff0)
    x, ctx_1024, mask_Bx1xSxS2_ik1, mask_Bx1x1xS2_ff0 = _rec_inputs()

    def _L0_xattn_setup():
        import jax, jax.numpy as jnp
        import numpy as np
        N, S, E, H = (4, 512, 256, 16)
        D = E // H
        key = jax.random.key(seed)
        ks = jax.random.split(key, 12)
        s = 1.0 / np.sqrt(E)
        inp = {'value': jax.random.normal(ks[0], (N, S, E), jnp.float32), 'key': jax.random.normal(ks[1], (N, S, E), jnp.float32), 'query': jax.random.normal(ks[2], (N, S, E), jnp.float32), 'mask': jax.random.randint(ks[3], (N, 1, S, S), 0, 2, dtype=jnp.int32), 'Wv': jax.random.normal(ks[4], (E, E), jnp.float32) * s, 'bv': jax.random.normal(ks[5], (E,), jnp.float32) * s, 'Wk': jax.random.normal(ks[6], (E, E), jnp.float32) * s, 'bk': jax.random.normal(ks[7], (E,), jnp.float32) * s, 'Wq': jax.random.normal(ks[8], (E, E), jnp.float32) * s, 'bq': jax.random.normal(ks[9], (E,), jnp.float32) * s, 'Wo': jax.random.normal(ks[10], (E, E), jnp.float32) * s, 'bo': jax.random.normal(ks[11], (E,), jnp.float32) * s}
        return inp
    _L0_xattn_all = _L0_xattn_setup()
    _L0_xattn_in = {k: v for k, v in _L0_xattn_all.items() if k in ('Wv', 'bv', 'Wk', 'bk', 'Wq', 'bq', 'Wo', 'bo')}
    del _L0_xattn_all

    def _L0_ffn_setup():
        import jax, jax.numpy as jnp
        import numpy as np
        H = 256
        I = 1024
        E = 4
        LN_EPS = 1e-12

        def _layer_norm(x, gamma, beta, eps=LN_EPS):
            mu = jnp.mean(x, axis=-1, keepdims=True)
            var = jnp.mean(jnp.square(x - mu), axis=-1, keepdims=True)
            return (x - mu) * jax.lax.rsqrt(var + eps) * gamma + beta
        key = jax.random.key(seed)
        ks = jax.random.split(key, 8)
        B, S = (4, 128)
        scale = 0.02
        return {'hidden_states': jax.random.normal(ks[0], (B, S, H), jnp.float32), 'W_router': jax.random.normal(ks[1], (H, E), jnp.float32) * scale, 'W1': jax.random.normal(ks[2], (E, H, I), jnp.float32) * scale, 'b1': jax.random.normal(ks[3], (E, I), jnp.float32) * scale, 'Wo': jax.random.normal(ks[4], (I, H), jnp.float32) * scale, 'bo': jax.random.normal(ks[5], (H,), jnp.float32) * scale, 'ln_gamma': jnp.ones((H,), jnp.float32), 'ln_beta': jnp.zeros((H,), jnp.float32)}
    _L0_ffn_all = _L0_ffn_setup()
    _L0_ffn_in = {k: v for k, v in _L0_ffn_all.items() if k in ('W_router', 'W1', 'b1', 'Wo', 'bo', 'ln_gamma', 'ln_beta')}
    del _L0_ffn_all

    def _L1_xattn_setup():
        import jax, jax.numpy as jnp
        import numpy as np
        H, D, DIM = (8, 128, 256)
        QB, N = (16, 128)

        def layer_norm(x, g, b, eps=1e-05):
            mu = x.mean(-1, keepdims=True)
            var = ((x - mu) ** 2).mean(-1, keepdims=True)
            return (x - mu) / jnp.sqrt(var + eps) * g + b
        key = jax.random.key(seed)
        ks = jax.random.split(key, 8)
        rn = lambda k, shape, s=1.0: jax.random.normal(k, shape, jnp.float32) * s
        return {'q': rn(ks[0], (QB, N, DIM)), 'k': rn(ks[1], (QB, N, DIM)), 'v': rn(ks[2], (QB, N, DIM)), 'ln_g': jnp.ones(DIM, jnp.float32), 'ln_b': jnp.zeros(DIM, jnp.float32), 'w_in': rn(ks[3], (H * D, DIM), 0.02), 'wp_w1': rn(ks[4], (D, 2 * D), 0.05), 'wp_b1': jnp.zeros(D, jnp.float32), 'wp_ln_g': jnp.ones(D, jnp.float32), 'wp_ln_b': jnp.zeros(D, jnp.float32), 'wp_w2': rn(ks[5], (3, D), 0.05), 'wp_b2': jnp.zeros(3, jnp.float32), 'w_out': rn(ks[6], (DIM, H * D), 0.02), 'b_out': jnp.zeros(DIM, jnp.float32)}
    _L1_xattn_all = _L1_xattn_setup()
    _L1_xattn_in = {k: v for k, v in _L1_xattn_all.items() if k in ('ln_g', 'ln_b', 'w_in', 'wp_w1', 'wp_b1', 'wp_ln_g', 'wp_ln_b', 'wp_w2', 'wp_b2', 'w_out', 'b_out')}
    del _L1_xattn_all

    def _L1_ffn_setup():
        import jax, jax.numpy as jnp
        import numpy as np
        import math
        E = 16
        TOP_K = 2
        D = 256
        F = 1024
        SH = 512
        key = jax.random.key(seed)
        ks = jax.random.split(key, 10)
        s = lambda k, shape, fan: jax.random.normal(k, shape, jnp.float32) / np.sqrt(fan)
        return {'x': jax.random.normal(ks[0], (32, 64, D), jnp.float32), 'gate_w': s(ks[1], (E, D), D), 'up_w': s(ks[2], (E, F, D), D), 'up_b': s(ks[3], (E, F), D), 'gw': s(ks[4], (E, F, D), D), 'gb': s(ks[5], (E, F), D), 'down_w': s(ks[6], (E, D, F), F), 'down_b': s(ks[7], (E, D), F), 'sh_gate_w': s(ks[8], (SH, D), D), 'sh_up_w': s(ks[9], (SH, D), D), 'sh_down_w': s(jax.random.fold_in(key, 11), (D, SH), SH)}
    _L1_ffn_all = _L1_ffn_setup()
    _L1_ffn_in = {k: v for k, v in _L1_ffn_all.items() if k in ('gate_w', 'up_w', 'up_b', 'gw', 'gb', 'down_w', 'down_b', 'sh_gate_w', 'sh_up_w', 'sh_down_w')}
    del _L1_ffn_all

    def _L2_xattn_setup():
        import jax, jax.numpy as jnp
        import numpy as np
        EMBED_DIM = 256
        NUM_HEADS = 16
        HEAD_DIM = EMBED_DIM // NUM_HEADS
        SCALE = HEAD_DIM ** (-0.5)
        key = jax.random.key(seed)
        ks = jax.random.split(key, 11)
        B, T, C = (4, 512, EMBED_DIM)
        s = 1.0 / np.sqrt(C)
        return {'query': jax.random.normal(ks[0], (B, T, C), jnp.float32), 'key': jax.random.normal(ks[1], (B, T, C), jnp.float32), 'value': jax.random.normal(ks[2], (B, T, C), jnp.float32), 'Wq': jax.random.normal(ks[3], (C, C), jnp.float32) * s, 'bq': jnp.zeros((C,), jnp.float32), 'Wk': jax.random.normal(ks[4], (C, C), jnp.float32) * s, 'bk': jnp.zeros((C,), jnp.float32), 'Wv': jax.random.normal(ks[5], (C, C), jnp.float32) * s, 'bv': jnp.zeros((C,), jnp.float32), 'Wo': jax.random.normal(ks[6], (C, C), jnp.float32) * s, 'bo': jnp.zeros((C,), jnp.float32)}
    _L2_xattn_all = _L2_xattn_setup()
    _L2_xattn_in = {k: v for k, v in _L2_xattn_all.items() if k in ('Wq', 'bq', 'Wk', 'bk', 'Wv', 'bv', 'Wo', 'bo')}
    del _L2_xattn_all

    def _L2_ffn_setup():
        import jax, jax.numpy as jnp
        import numpy as np
        MANT_BITS = 8
        _PWL_X = jnp.linspace(-4.0, 4.0, 33, dtype=jnp.float32)
        _PWL_Y = 0.5 * _PWL_X * (1.0 + jax.lax.erf(_PWL_X / jnp.sqrt(jnp.float32(2.0))))

        def float2fix(x, mantissa_bits):
            s = jnp.float32(2.0 ** mantissa_bits)
            q = jnp.round(x * s) / s
            return x + jax.lax.stop_gradient(q - x)

        def pwlin_gelu_basic(x, mantissa_bits_in, mantissa_bits_out):
            xq = float2fix(x, mantissa_bits_in)
            y = jnp.interp(xq, _PWL_X, _PWL_Y)
            y = jnp.where(xq > 4.0, xq, jnp.where(xq < -4.0, jnp.float32(0.0), y))
            return float2fix(y, mantissa_bits_out)
        key = jax.random.key(seed)
        k_x, k_w1, k_b1, k_w2, k_b2 = jax.random.split(key, 5)
        dim, ff_dim = (256, 1024)
        B, S = (32, 128)
        sc1 = 1.0 / np.sqrt(dim)
        sc2 = 1.0 / np.sqrt(ff_dim)
        return {'x': jax.random.normal(k_x, (B, S, dim), dtype=jnp.float32), 'w1': jax.random.uniform(k_w1, (dim, ff_dim), jnp.float32, -sc1, sc1), 'b1': jax.random.uniform(k_b1, (ff_dim,), jnp.float32, -sc1, sc1), 'w2': jax.random.uniform(k_w2, (ff_dim, dim), jnp.float32, -sc2, sc2), 'b2': jax.random.uniform(k_b2, (dim,), jnp.float32, -sc2, sc2)}
    _L2_ffn_all = _L2_ffn_setup()
    _L2_ffn_in = {k: v for k, v in _L2_ffn_all.items() if k in ('w1', 'b1', 'w2', 'b2')}
    del _L2_ffn_all

    def _L3_xattn_setup():
        import jax, jax.numpy as jnp
        import numpy as np
        N_HEAD = 16

        def _split_heads(t):
            B, S, D = t.shape
            return t.reshape(B, S, N_HEAD, D // N_HEAD).transpose(0, 2, 1, 3)
        key = jax.random.key(seed)
        ks = jax.random.split(key, 8)
        B, Sq, Sk, D = (4, 256, 512, 256)
        s = 0.02
        return {'x': jax.random.normal(ks[0], (B, Sq, D), jnp.float32), 'ctx': jax.random.normal(ks[1], (B, Sk, D), jnp.float32), 'attention_mask': jnp.zeros((B, 1, 1, Sk), jnp.float32), 'Wq': jax.random.normal(ks[2], (D, D), jnp.float32) * s, 'bq': jnp.zeros((D,), jnp.float32), 'Wkv': jax.random.normal(ks[3], (D, 2 * D), jnp.float32) * s, 'bkv': jnp.zeros((2 * D,), jnp.float32), 'Wp': jax.random.normal(ks[4], (D, D), jnp.float32) * s, 'bp': jnp.zeros((D,), jnp.float32)}
    _L3_xattn_all = _L3_xattn_setup()
    _L3_xattn_in = {k: v for k, v in _L3_xattn_all.items() if k in ('Wq', 'bq', 'Wkv', 'bkv', 'Wp', 'bp')}
    del _L3_xattn_all

    def _L3_ffn_setup():
        import jax, jax.numpy as jnp
        import numpy as np
        key = jax.random.key(seed)
        k1, k2, k3 = jax.random.split(key, 3)
        B, S, D, E, H = (4, 512, 256, 8, 256)
        x = jax.random.normal(k1, (B, S, D), dtype=jnp.float32)
        Wg = jax.random.normal(k2, (D, E), dtype=jnp.float32) / np.sqrt(D)
        We = jax.random.normal(k3, (E, D, H), dtype=jnp.float32) / np.sqrt(D)
        be = jnp.zeros((E, H), dtype=jnp.float32)
        return {'x': x, 'Wg': Wg, 'We': We, 'be': be}
    _L3_ffn_all = _L3_ffn_setup()
    _L3_ffn_in = {k: v for k, v in _L3_ffn_all.items() if k in ('Wg', 'We', 'be')}
    del _L3_ffn_all
    return {'x': x, 'ctx_1024': ctx_1024, 'mask_Bx1xSxS2_ik1': mask_Bx1xSxS2_ik1, 'mask_Bx1x1xS2_ff0': mask_Bx1x1xS2_ff0, 'L0_xattn_Wv': _L0_xattn_in['Wv'], 'L0_xattn_bv': _L0_xattn_in['bv'], 'L0_xattn_Wk': _L0_xattn_in['Wk'], 'L0_xattn_bk': _L0_xattn_in['bk'], 'L0_xattn_Wq': _L0_xattn_in['Wq'], 'L0_xattn_bq': _L0_xattn_in['bq'], 'L0_xattn_Wo': _L0_xattn_in['Wo'], 'L0_xattn_bo': _L0_xattn_in['bo'], 'L0_ffn_W_router': _L0_ffn_in['W_router'], 'L0_ffn_W1': _L0_ffn_in['W1'], 'L0_ffn_b1': _L0_ffn_in['b1'], 'L0_ffn_Wo': _L0_ffn_in['Wo'], 'L0_ffn_bo': _L0_ffn_in['bo'], 'L0_ffn_ln_gamma': _L0_ffn_in['ln_gamma'], 'L0_ffn_ln_beta': _L0_ffn_in['ln_beta'], 'L1_xattn_ln_g': _L1_xattn_in['ln_g'], 'L1_xattn_ln_b': _L1_xattn_in['ln_b'], 'L1_xattn_w_in': _L1_xattn_in['w_in'], 'L1_xattn_wp_w1': _L1_xattn_in['wp_w1'], 'L1_xattn_wp_b1': _L1_xattn_in['wp_b1'], 'L1_xattn_wp_ln_g': _L1_xattn_in['wp_ln_g'], 'L1_xattn_wp_ln_b': _L1_xattn_in['wp_ln_b'], 'L1_xattn_wp_w2': _L1_xattn_in['wp_w2'], 'L1_xattn_wp_b2': _L1_xattn_in['wp_b2'], 'L1_xattn_w_out': _L1_xattn_in['w_out'], 'L1_xattn_b_out': _L1_xattn_in['b_out'], 'L1_ffn_gate_w': _L1_ffn_in['gate_w'], 'L1_ffn_up_w': _L1_ffn_in['up_w'], 'L1_ffn_up_b': _L1_ffn_in['up_b'], 'L1_ffn_gw': _L1_ffn_in['gw'], 'L1_ffn_gb': _L1_ffn_in['gb'], 'L1_ffn_down_w': _L1_ffn_in['down_w'], 'L1_ffn_down_b': _L1_ffn_in['down_b'], 'L1_ffn_sh_gate_w': _L1_ffn_in['sh_gate_w'], 'L1_ffn_sh_up_w': _L1_ffn_in['sh_up_w'], 'L1_ffn_sh_down_w': _L1_ffn_in['sh_down_w'], 'L2_xattn_Wq': _L2_xattn_in['Wq'], 'L2_xattn_bq': _L2_xattn_in['bq'], 'L2_xattn_Wk': _L2_xattn_in['Wk'], 'L2_xattn_bk': _L2_xattn_in['bk'], 'L2_xattn_Wv': _L2_xattn_in['Wv'], 'L2_xattn_bv': _L2_xattn_in['bv'], 'L2_xattn_Wo': _L2_xattn_in['Wo'], 'L2_xattn_bo': _L2_xattn_in['bo'], 'L2_ffn_w1': _L2_ffn_in['w1'], 'L2_ffn_b1': _L2_ffn_in['b1'], 'L2_ffn_w2': _L2_ffn_in['w2'], 'L2_ffn_b2': _L2_ffn_in['b2'], 'L3_xattn_Wq': _L3_xattn_in['Wq'], 'L3_xattn_bq': _L3_xattn_in['bq'], 'L3_xattn_Wkv': _L3_xattn_in['Wkv'], 'L3_xattn_bkv': _L3_xattn_in['bkv'], 'L3_xattn_Wp': _L3_xattn_in['Wp'], 'L3_xattn_bp': _L3_xattn_in['bp'], 'L3_ffn_Wg': _L3_ffn_in['Wg'], 'L3_ffn_We': _L3_ffn_in['We'], 'L3_ffn_be': _L3_ffn_in['be']}

def reference(x, ctx_1024, mask_Bx1xSxS2_ik1, mask_Bx1x1xS2_ff0, L0_xattn_Wv, L0_xattn_bv, L0_xattn_Wk, L0_xattn_bk, L0_xattn_Wq, L0_xattn_bq, L0_xattn_Wo, L0_xattn_bo, L0_ffn_W_router, L0_ffn_W1, L0_ffn_b1, L0_ffn_Wo, L0_ffn_bo, L0_ffn_ln_gamma, L0_ffn_ln_beta, L1_xattn_ln_g, L1_xattn_ln_b, L1_xattn_w_in, L1_xattn_wp_w1, L1_xattn_wp_b1, L1_xattn_wp_ln_g, L1_xattn_wp_ln_b, L1_xattn_wp_w2, L1_xattn_wp_b2, L1_xattn_w_out, L1_xattn_b_out, L1_ffn_gate_w, L1_ffn_up_w, L1_ffn_up_b, L1_ffn_gw, L1_ffn_gb, L1_ffn_down_w, L1_ffn_down_b, L1_ffn_sh_gate_w, L1_ffn_sh_up_w, L1_ffn_sh_down_w, L2_xattn_Wq, L2_xattn_bq, L2_xattn_Wk, L2_xattn_bk, L2_xattn_Wv, L2_xattn_bv, L2_xattn_Wo, L2_xattn_bo, L2_ffn_w1, L2_ffn_b1, L2_ffn_w2, L2_ffn_b2, L3_xattn_Wq, L3_xattn_bq, L3_xattn_Wkv, L3_xattn_bkv, L3_xattn_Wp, L3_xattn_bp, L3_ffn_Wg, L3_ffn_We, L3_ffn_be):
    import jax
    import jax.numpy as jnp

    def _L0_xattn_ref(value, key, query, mask, Wv, bv, Wk, bk, Wq, bq, Wo, bo):
        import jax, jax.numpy as jnp
        import numpy as np
        N, S, E, H = (4, 512, 256, 16)
        D = E // H
        n, q_len = (query.shape[0], query.shape[1])
        v = (value @ Wv.T + bv).reshape(n, -1, H, D)
        k = (key @ Wk.T + bk).reshape(n, -1, H, D)
        q = (query @ Wq.T + bq).reshape(n, -1, H, D)
        qk = jnp.einsum('nqhd,nkhd->nhqk', q, k)
        qk = jnp.where(mask == 0, jnp.asarray(1e-20, qk.dtype), qk)
        attn = jax.nn.softmax(qk / jnp.asarray(np.sqrt(E), qk.dtype), axis=3)
        out = jnp.einsum('nhqk,nkhd->nqhd', attn, v).reshape(n, q_len, H * D)
        return out @ Wo.T + bo

    def _L0_ffn_ref(hidden_states, W_router, W1, b1, Wo, bo, ln_gamma, ln_beta):
        import jax, jax.numpy as jnp
        import numpy as np
        H = 256
        I = 1024
        E = 4
        LN_EPS = 1e-12

        def _layer_norm(x, gamma, beta, eps=LN_EPS):
            mu = jnp.mean(x, axis=-1, keepdims=True)
            var = jnp.mean(jnp.square(x - mu), axis=-1, keepdims=True)
            return (x - mu) * jax.lax.rsqrt(var + eps) * gamma + beta
        B, S, _ = hidden_states.shape
        x = hidden_states.reshape(-1, H)
        logits = x @ W_router
        expert_idx = jnp.argmax(logits, axis=-1)
        h = jnp.einsum('th,ehi->tei', x, W1) + b1
        h = jax.nn.gelu(h, approximate=False)
        onehot = jax.nn.one_hot(expert_idx, E, dtype=x.dtype)
        intermediate = jnp.einsum('te,tei->ti', onehot, h)
        y = intermediate @ Wo + bo + x
        y = _layer_norm(y, ln_gamma, ln_beta)
        return y.reshape(B, S, H)

    def _L1_xattn_ref(q, k, v, ln_g, ln_b, w_in, wp_w1, wp_b1, wp_ln_g, wp_ln_b, wp_w2, wp_b2, w_out, b_out):
        import jax, jax.numpy as jnp
        import numpy as np
        H, D, DIM = (8, 128, 256)
        QB, N = (16, 128)

        def layer_norm(x, g, b, eps=1e-05):
            mu = x.mean(-1, keepdims=True)
            var = ((x - mu) ** 2).mean(-1, keepdims=True)
            return (x - mu) / jnp.sqrt(var + eps) * g + b

        def proj(t):
            x = layer_norm(t, ln_g, ln_b) @ w_in.T
            Qd, Nd = (t.shape[0], t.shape[1])
            return x.reshape(Qd, Nd, H, D).transpose(2, 0, 1, 3)
        f_q, f_k, f_v = (proj(q), proj(k), proj(v))
        dots = jnp.einsum('hqnd,hqmd->hqnm', f_q, f_k)
        qn = jnp.linalg.norm(f_q, axis=-1)
        kn = jnp.linalg.norm(f_k, axis=-1)
        cosine_sim = dots / (qn[..., :, None] * kn[..., None, :])
        q_centered = f_q - f_q.mean(-1, keepdims=True)
        q_var = jnp.var(f_q, axis=-1, ddof=1)
        k_var = jnp.var(f_k, axis=-1, ddof=1)
        q_ratio = 2.0 * jnp.minimum(q_var, 1.0) / (q_var + 1.0)
        k_ratio = 2.0 * jnp.minimum(k_var, 1.0) / (k_var + 1.0)
        var_component = jnp.einsum('hqn,hqm->hqnm', q_ratio, k_ratio)
        q_flat = q_centered.reshape(H, -1, D)
        feat_corr = jnp.einsum('hnd,hne->hde', q_flat, q_flat) / q_flat.shape[1]
        feat_corr = feat_corr * (1.0 - jnp.eye(D, dtype=feat_corr.dtype))
        decorr_score = jnp.linalg.norm(feat_corr, axis=(-2, -1)) / (D * D)
        decorr_scale = jnp.exp(-5.0 * decorr_score)[:, None, None, None]
        cov_component = cosine_sim * decorr_scale
        q_global = f_q.mean(axis=(1, 2))
        k_global = f_k.mean(axis=(1, 2))
        feats = jnp.concatenate([q_global, k_global], axis=-1)
        h1 = jnp.maximum(layer_norm(feats @ wp_w1.T + wp_b1, wp_ln_g, wp_ln_b), 0.0)
        weights = jax.nn.softmax(h1 @ wp_w2.T + wp_b2, axis=-1)
        cw = weights[:, 0][:, None, None, None]
        vw = weights[:, 1][:, None, None, None]
        ww = weights[:, 2][:, None, None, None]
        mixed = cw * cosine_sim + vw * cov_component + ww * var_component
        out = jnp.einsum('hqnm,hqmd->hqnd', mixed, f_v)
        out = out.transpose(1, 2, 0, 3).reshape(q.shape[0], q.shape[1], H * D)
        return out @ w_out.T + b_out

    def _L1_ffn_ref(x, gate_w, up_w, up_b, gw, gb, down_w, down_b, sh_gate_w, sh_up_w, sh_down_w):
        import jax, jax.numpy as jnp
        import numpy as np
        import math
        E = 16
        TOP_K = 2
        D = 256
        F = 1024
        SH = 512
        B, S, Dm = x.shape
        h = x.reshape(-1, Dm)
        T = h.shape[0]
        scores = jax.nn.sigmoid(h @ gate_w.T)
        cap = math.ceil(T / E * TOP_K)
        topk_score, topk_ids = jax.lax.top_k(scores.T, cap)
        xin = h[topk_ids]
        up = jnp.einsum('ecd,efd->ecf', xin, up_w) + up_b[:, None, :]
        g = jnp.einsum('ecd,efd->ecf', xin, gw) + gb[:, None, :]
        eo = jax.nn.silu(g) * up
        eo = jnp.einsum('ecf,edf->ecd', eo, down_w) + down_b[:, None, :]
        flat = (eo * topk_score[..., None]).reshape(-1, Dm)
        out = jnp.zeros_like(h).at[topk_ids.reshape(-1)].add(flat)
        out = out.reshape(B, S, Dm)
        shared = jax.nn.silu(jnp.einsum('bsd,fd->bsf', x, sh_gate_w)) * jnp.einsum('bsd,fd->bsf', x, sh_up_w)
        shared = jnp.einsum('bsf,df->bsd', shared, sh_down_w)
        return out + shared

    def _L2_xattn_ref(query, key, value, Wq, bq, Wk, bk, Wv, bv, Wo, bo):
        import jax, jax.numpy as jnp
        import numpy as np
        EMBED_DIM = 256
        NUM_HEADS = 16
        HEAD_DIM = EMBED_DIM // NUM_HEADS
        SCALE = HEAD_DIM ** (-0.5)
        B, Tq, C = query.shape
        Tk = key.shape[1]
        H, D = (NUM_HEADS, HEAD_DIM)
        q = (query @ Wq.T + bq).reshape(B, Tq, H, D).transpose(0, 2, 1, 3)
        k = (key @ Wk.T + bk).reshape(B, Tk, H, D).transpose(0, 2, 1, 3)
        v = (value @ Wv.T + bv).reshape(B, Tk, H, D).transpose(0, 2, 1, 3)
        scores = jnp.einsum('bhqd,bhkd->bhqk', q, k) * SCALE
        attn = jax.nn.softmax(scores, axis=-1)
        out = jnp.einsum('bhqk,bhkd->bhqd', attn, v)
        out = out.transpose(0, 2, 1, 3).reshape(B, Tq, C)
        return out @ Wo.T + bo

    def _L2_ffn_ref(x, w1, b1, w2, b2):
        import jax, jax.numpy as jnp
        import numpy as np
        MANT_BITS = 8
        _PWL_X = jnp.linspace(-4.0, 4.0, 33, dtype=jnp.float32)
        _PWL_Y = 0.5 * _PWL_X * (1.0 + jax.lax.erf(_PWL_X / jnp.sqrt(jnp.float32(2.0))))

        def float2fix(x, mantissa_bits):
            s = jnp.float32(2.0 ** mantissa_bits)
            q = jnp.round(x * s) / s
            return x + jax.lax.stop_gradient(q - x)

        def pwlin_gelu_basic(x, mantissa_bits_in, mantissa_bits_out):
            xq = float2fix(x, mantissa_bits_in)
            y = jnp.interp(xq, _PWL_X, _PWL_Y)
            y = jnp.where(xq > 4.0, xq, jnp.where(xq < -4.0, jnp.float32(0.0), y))
            return float2fix(y, mantissa_bits_out)
        h = jnp.einsum('bsd,df->bsf', x, w1) + b1
        h = float2fix(h, MANT_BITS)
        h = pwlin_gelu_basic(h, MANT_BITS, MANT_BITS)
        h = float2fix(h, MANT_BITS)
        out = jnp.einsum('bsf,fd->bsd', h, w2) + b2
        return float2fix(out, MANT_BITS)

    def _L3_xattn_ref(x, ctx, attention_mask, Wq, bq, Wkv, bkv, Wp, bp):
        import jax, jax.numpy as jnp
        import numpy as np
        N_HEAD = 16

        def _split_heads(t):
            B, S, D = t.shape
            return t.reshape(B, S, N_HEAD, D // N_HEAD).transpose(0, 2, 1, 3)
        B, Sq, D = x.shape
        dh = D // N_HEAD
        q = _split_heads(x @ Wq + bq)
        kv = ctx @ Wkv + bkv
        k = _split_heads(kv[..., :D])
        v = _split_heads(kv[..., D:])
        w = jnp.einsum('bhqd,bhkd->bhqk', q, k) / jnp.sqrt(jnp.float32(dh))
        w = w + attention_mask
        w = jax.nn.softmax(w, axis=-1)
        a = jnp.einsum('bhqk,bhkd->bhqd', w, v)
        a = a.transpose(0, 2, 1, 3).reshape(B, Sq, D)
        return a @ Wp + bp

    def _L3_ffn_ref(x, Wg, We, be):
        import jax, jax.numpy as jnp
        import numpy as np
        B, S, D = x.shape
        E = Wg.shape[1]
        T = B * S
        xf = x.reshape(T, D)
        gates = jax.nn.softmax(xf @ Wg, axis=-1)
        top_g, top_i = jax.lax.top_k(gates, 2)
        top_g = top_g / jnp.sum(top_g, axis=-1, keepdims=True)
        tok = jnp.arange(T)
        dispatch = jnp.zeros((E, T), dtype=gates.dtype)
        for i in range(2):
            dispatch = dispatch.at[top_i[:, i], tok].add(top_g[:, i])
        y = jnp.einsum('td,edh->eth', xf, We) + be[:, None, :]
        out = jnp.einsum('et,eth->th', dispatch, y)
        return out.reshape(B, S, -1)
    x = x + _L0_xattn_ref(ctx_1024, ctx_1024, _layernorm(x, axis=-1), mask_Bx1xSxS2_ik1, L0_xattn_Wv, L0_xattn_bv, L0_xattn_Wk, L0_xattn_bk, L0_xattn_Wq, L0_xattn_bq, L0_xattn_Wo, L0_xattn_bo)
    x = x + _L0_ffn_ref(_layernorm(x, axis=-1), L0_ffn_W_router, L0_ffn_W1, L0_ffn_b1, L0_ffn_Wo, L0_ffn_bo, L0_ffn_ln_gamma, L0_ffn_ln_beta)
    x = x + _L1_xattn_ref(_layernorm(x, axis=-1), ctx_1024, ctx_1024, L1_xattn_ln_g, L1_xattn_ln_b, L1_xattn_w_in, L1_xattn_wp_w1, L1_xattn_wp_b1, L1_xattn_wp_ln_g, L1_xattn_wp_ln_b, L1_xattn_wp_w2, L1_xattn_wp_b2, L1_xattn_w_out, L1_xattn_b_out)
    x = x + _L1_ffn_ref(_layernorm(x, axis=-1), L1_ffn_gate_w, L1_ffn_up_w, L1_ffn_up_b, L1_ffn_gw, L1_ffn_gb, L1_ffn_down_w, L1_ffn_down_b, L1_ffn_sh_gate_w, L1_ffn_sh_up_w, L1_ffn_sh_down_w)
    x = x + _L2_xattn_ref(_layernorm(x, axis=-1), ctx_1024, ctx_1024, L2_xattn_Wq, L2_xattn_bq, L2_xattn_Wk, L2_xattn_bk, L2_xattn_Wv, L2_xattn_bv, L2_xattn_Wo, L2_xattn_bo)
    x = x + _L2_ffn_ref(_layernorm(x, axis=-1), L2_ffn_w1, L2_ffn_b1, L2_ffn_w2, L2_ffn_b2)
    x = x + _L3_xattn_ref(_layernorm(x, axis=-1), ctx_1024, mask_Bx1x1xS2_ff0, L3_xattn_Wq, L3_xattn_bq, L3_xattn_Wkv, L3_xattn_bkv, L3_xattn_Wp, L3_xattn_bp)
    x = x + _L3_ffn_ref(_layernorm(x, axis=-1), L3_ffn_Wg, L3_ffn_We, L3_ffn_be)
    return x

_drawn_inputs = setup_inputs


def setup_inputs(seed=0):
    import zlib

    import numpy as np

    out = dict(_drawn_inputs(seed))
    spreads = {'L0_ffn_ln_gamma': (1.0, 0.2),
     'L0_ffn_ln_beta': (0.0, 0.1),
     'L1_xattn_ln_g': (1.0, 0.2),
     'L1_xattn_ln_b': (0.0, 0.1),
     'L1_xattn_wp_b1': (0.0, 0.1),
     'L1_xattn_wp_ln_g': (1.0, 0.2),
     'L1_xattn_wp_ln_b': (0.0, 0.1),
     'L1_xattn_wp_b2': (0.0, 0.1),
     'L1_xattn_b_out': (0.0, 0.1),
     'L2_xattn_bq': (0.0, 0.656),
     'L2_xattn_bk': (0.0, 2.0),
     'L2_xattn_bv': (0.0, 0.1),
     'L2_xattn_bo': (0.0, 0.1),
     'L3_xattn_bq': (0.0, 2.0),
     'L3_xattn_bkv': (0.0, 0.477),
     'L3_xattn_bp': (0.0, 0.1),
     'L3_ffn_be': (0.0, 0.432)}
    factors = {'L0_xattn_bk': 46.111,
     'L0_xattn_bq': 4.871,
     'L0_ffn_b1': 3.97,
     'L1_ffn_up_b': 3.305,
     'L1_ffn_gb': 3.342,
     'L1_ffn_down_b': 3.803,
     'L2_ffn_b1': 7.878,
     'L2_ffn_b2': 6.392,
     'L3_xattn_Wq': 8.0,
     'L3_xattn_Wkv': 2.866}
    for name, (base, spread) in spreads.items():
        noise = np.random.default_rng([zlib.crc32(name.encode()), seed]).standard_normal(out[name].shape)
        drawn = base * np.exp(spread * noise) if base else spread * noise
        out[name] = jnp.asarray(drawn.astype(out[name].dtype))
    for name, factor in factors.items():
        out[name] = (out[name] * factor).astype(out[name].dtype)
    return out
```

```python
from contextlib import ExitStack, contextmanager

import concourse.bass as bass
from concourse import mybir
from concourse.alu_op_type import AluOpType as ALU

ACT = mybir.ActivationFunctionType
F32 = mybir.dt.float32
BF16 = mybir.dt.bfloat16
I32 = mybir.dt.int32
U32 = mybir.dt.uint32
AX_X = mybir.AxisListType.X

P = 128
B = 8
S = 512
D = 256
N_TOK = B * S
TB = S // P
NT = N_TOK // P
KD = D // P
LN_EPS = 1e-5
ROUNDER = 1.5 * 2.0**23



class Shared:
    pass

def batch_loop(nc, count, sems, build_body):
    with nc.Fori(0, count) as b:
        with nc.Block() as block:
            build_body(block, b)
        for s in sems:
            nc.sync.sem_clear(s)
        nc.all_engine_barrier()


@contextmanager
def stage_semaphores(nc, prefix):
    taken = []
    with ExitStack() as held:
        def sem(name):
            taken.append(held.enter_context(nc.semaphore(prefix + name)))
            return taken[-1]

        yield sem
        for s in taken:
            nc.sync.sem_clear(s)
        nc.all_engine_barrier()


def chained(eng, sem):
    count = [0]

    def link(ins):
        count[0] += 1
        ins.then_inc(sem, 1)
        eng.wait_ge(sem, count[0])

    return link


def load_weights(nc, loads, done):
    with nc.Block() as block:
        @block.sync
        def _(sp):
            for tile, src in loads:
                sp.dma_start(tile, src).then_inc(done, 16)
            sp.wait_ge(done, 16 * len(loads))


def bcast_row(vector):
    return vector.rearrange("(a n) -> a n", a=1).partition_broadcast(P)



def front_buffers(nc, ctx, prefix):
    sb = lambda n, s, d=F32: ctx.enter_context(nc.sbuf_tensor(prefix + n, s, d))
    sem = ctx.enter_context(stage_semaphores(nc, prefix))
    f = Shared()
    f.stats = sb("stats", [P, TB, 6])
    f.meanvar = sb("meanvar", [P, TB, 2])
    f.var = sb("var", [P, TB])
    f.std = sb("std", [P, TB])
    f.rstd = sb("rstd", [P, TB])
    f.xn = sb("xn", [P, TB, D])
    f.xT = sb("xT", [P, KD, S])
    f.var_ready, f.std_ready, f.xn_ready = sem("var_ready"), sem("std_ready"), sem("xn_ready")
    f.xT_in_psum, f.xT_ready = sem("xT_in_psum"), sem("xT_ready")
    f.sems = [f.var_ready, f.std_ready, f.xn_ready, f.xT_in_psum, f.xT_ready]
    return f


def ln_stats(nc, link, f, tile_of, eps):
    for t in range(TB):
        last = nc.vector.bn_stats(f.stats[:, t, :], tile_of(t))
    link(last)
    for t in range(TB):
        last = nc.vector.bn_aggr(f.meanvar[:, t, :], f.stats[:, t, :])
    link(last)
    nc.vector.tensor_scalar(f.var[:], f.meanvar[:, :, 1], eps, None, ALU.add).then_inc(f.var_ready, 1)


def ln_apply(nc, dve, link, f, tile_of, done=1):
    dve.wait_ge(f.std_ready, done)
    link(nc.vector.reciprocal(f.rstd[:], f.std[:]))
    for t in range(TB):
        nc.vector.tensor_scalar(f.xn[:, t, :], tile_of(t), f.meanvar[:, t, 0:1], f.rstd[:, t:t + 1],
                                ALU.subtract, ALU.mult).then_inc(f.xn_ready, 1)


def ln_roots(nc, act, f, done=1):
    act.wait_ge(f.var_ready, done)
    nc.scalar.activation(f.std[:], f.var[:], ACT.Sqrt).then_inc(f.std_ready, 1)


def transpose_tokens(nc, pe, src, psT, ident, ready, base, done):
    for t in range(TB):
        pe.wait_ge(ready, base + t + 1)
        for k in range(KD):
            last = nc.tensor.transpose(psT[:, k, t * P:(t + 1) * P], src[:, t, k * P:(k + 1) * P], ident[:])
    last.then_inc(done, 1)



def moe_top2(nc, A, G):
    E = 8
    with ExitStack() as ctx:
        sb = lambda n, s, d=F32: ctx.enter_context(nc.sbuf_tensor("m3_" + n, s, d))
        psum = lambda n, s, d=F32: ctx.enter_context(nc.psum_tensor("m3_" + n, s, d))
        sem = ctx.enter_context(stage_semaphores(nc, "m3_"))
        f = front_buffers(nc, ctx, "m3_")
        wg = sb("wg", [P, KD, E])
        we = sb("we", [P, KD, E, D])
        be = sb("be", [E, D])
        lower = sb("lower", [P, E, E])
        mx, nmx, z, rz = sb("mx", [P, TB]), sb("nmx", [P, TB]), sb("z", [P, TB]), sb("rz", [P, TB])
        ex, gate = sb("ex", [P, TB, E]), sb("gate", [P, TB, E])
        cmp, eq = sb("cmp", [P, TB, E, E]), sb("eq", [P, TB, E, E])
        rank = sb("rank", [P, TB, E])
        picked, total, rtotal = sb("picked", [P, TB, E]), sb("total", [P, TB]), sb("rtotal", [P, TB])
        disp = sb("disp", [P, TB, E])
        dispT = sb("dispT", [E, S])
        psT = psum("psT", [P, KD, S])
        psG = psum("psG", [P, S])
        psY = psum("psY", [P, 4, S])
        loaded, lower_set = sem("loaded"), sem("lower_set")
        logits_ready, shifted, exp_ready, disp_ready = sem("logits_ready"), sem("shifted"), sem("exp_ready"), sem("disp_ready")
        dispT_in_psum, dispT_ready = sem("dispT_in_psum"), sem("dispT_ready")
        bias_ready = sem("bias_ready")
        y_ready, y_used = sem("y_ready"), sem("y_used")
        chain = sem("chain")
        sems = [*f.sems, logits_ready, shifted, exp_ready, disp_ready, dispT_in_psum, dispT_ready,
                bias_ready, y_ready, y_used, chain]

        loads = [(wg[:], A["L3_ffn_Wg"].rearrange("(k p) e -> p k e", p=P)), (be[:], A["L3_ffn_be"])]
        loads += [(we[:, k], A["L3_ffn_We"][:, k * P:(k + 1) * P, :].rearrange("e p h -> p e h")) for k in range(KD)]
        load_weights(nc, loads, loaded)
        lower_triangle(nc, lower, E, lower_set)

        def body(block, b):
            tile = lambda t: G.X[:, b * TB + t, :]

            @block.tensor
            def _(pe):
                transpose_tokens(nc, pe, f.xn, psT, G.ident, f.xn_ready, 0, f.xT_in_psum)
                pe.wait_ge(f.xT_ready, 1)
                for t in range(TB):
                    for k in range(KD):
                        last = nc.tensor.matmul(psG[:, t * E:(t + 1) * E], f.xT[:, k, t * P:(t + 1) * P], wg[:, k, :],
                                                start=(k == 0), stop=(k == KD - 1))
                last.then_inc(logits_ready, 1)
                n = 0
                for t in range(TB):
                    for j in range(4):
                        if n >= 4:
                            pe.wait_ge(y_used, n - 3)
                        for k in range(KD):
                            last = nc.tensor.matmul(psY[:, n % 4, :], f.xT[:, k, t * P:(t + 1) * P],
                                                    we[:, k, 2 * j:2 * j + 2, :], start=(k == 0), stop=(k == KD - 1))
                        last.then_inc(y_ready, 1)
                        n += 1
                        if n == 3:
                            pe.wait_ge(disp_ready, 1)
                            for u in range(TB):
                                last = nc.tensor.transpose(psG[0:E, u * P:(u + 1) * P], disp[:, u, :], G.ident[:])
                            last.then_inc(dispT_in_psum, 1)
                            pe.wait_ge(dispT_ready, 1)
                            for u in range(TB):
                                last = nc.tensor.matmul(psT[:, u // 2, (u % 2) * D:(u % 2 + 1) * D],
                                                        dispT[:, u * P:(u + 1) * P], be[:], start=True, stop=True)
                            last.then_inc(bias_ready, 1)

            @block.scalar
            def _(act):
                ln_roots(nc, act, f)
                act.wait_ge(f.xT_in_psum, 1)
                nc.scalar.copy(f.xT[:], psT[:]).then_inc(f.xT_ready, 1)
                act.wait_ge(shifted, 1)
                nc.scalar.activation(ex[:], gate[:], ACT.Exp).then_inc(exp_ready, 1)
                act.wait_ge(dispT_in_psum, 1)
                nc.scalar.copy(dispT[:], psG[0:E, :]).then_inc(dispT_ready, 1)

            @block.vector
            def _(dve):
                link = chained(dve, chain)
                ln_stats(nc, link, f, tile, LN_EPS)
                ln_apply(nc, dve, link, f, tile)
                dve.wait_ge(logits_ready, 1)
                logits = psG[:, 0:TB * E].rearrange("p (t e) -> p t e", e=E)
                link(nc.vector.tensor_reduce(mx[:], logits, AX_X, ALU.max))
                nc.vector.tensor_tensor(gate[:], logits, mx[:].unsqueeze(2).to_broadcast([P, TB, E]),
                                        ALU.subtract).then_inc(shifted, 1)
                dve.wait_ge(exp_ready, 1)
                link(nc.vector.tensor_reduce(z[:], ex[:], AX_X, ALU.add))
                link(nc.vector.reciprocal(rz[:], z[:]))
                link(nc.vector.tensor_tensor(gate[:], ex[:], rz[:].unsqueeze(2).to_broadcast([P, TB, E]), ALU.mult))
                rank_experts(nc, link, gate, rank, cmp, eq, lower, E)
                link(nc.vector.scalar_tensor_tensor(picked[:], rank[:], 2.0, gate[:], ALU.is_lt, ALU.mult))
                link(nc.vector.tensor_reduce(total[:], picked[:], AX_X, ALU.add))
                link(nc.vector.reciprocal(rtotal[:], total[:]))
                nc.vector.tensor_tensor(disp[:], picked[:], rtotal[:].unsqueeze(2).to_broadcast([P, TB, E]),
                                        ALU.mult).then_inc(disp_ready, 1)
                dve.wait_ge(bias_ready, 1)
                for t in range(TB):
                    last = nc.vector.tensor_tensor(tile(t), tile(t), psT[:, t // 2, (t % 2) * D:(t % 2 + 1) * D], ALU.add)
                link(last)
                for n in range(4 * TB):
                    t, j = n // 4, n % 4
                    dve.wait_ge(y_ready, n + 1)
                    link(nc.vector.scalar_tensor_tensor(tile(t), psY[:, n % 4, 0:D], disp[:, t, 2 * j:2 * j + 1],
                                                        tile(t), ALU.mult, ALU.add))
                    nc.vector.scalar_tensor_tensor(tile(t), psY[:, n % 4, D:], disp[:, t, 2 * j + 1:2 * j + 2],
                                                   tile(t), ALU.mult, ALU.add).then_inc(y_used, 1)
                    dve.wait_ge(y_used, n + 1)

        batch_loop(nc, B, sems, body)


def lower_triangle(nc, lower, E, lower_set):
    with nc.Block() as block:
        @block.gpsimd
        def _(pool):
            nc.gpsimd.memset(lower[:], 1.0).then_inc(lower_set, 1)
            pool.wait_ge(lower_set, 1)
            nc.gpsimd.affine_select(out=lower[:], in_=lower[:], compare_op=ALU.is_gt, fill=0.0, base=0,
                                    pattern=[[1, E], [-1, E]], channel_multiplier=0).then_inc(lower_set, 1)
            pool.wait_ge(lower_set, 2)


def rank_experts(nc, link, score, rank, cmp, eq, lower, E):
    for t in range(TB):
        rows = score[:, t, :].unsqueeze(1).to_broadcast([P, E, E])
        cols = score[:, t, :].unsqueeze(2).to_broadcast([P, E, E])
        nc.vector.tensor_tensor(cmp[:, t], rows, cols, ALU.is_gt)
        last = nc.vector.tensor_tensor(eq[:, t], rows, cols, ALU.is_equal)
    link(last)
    for t in range(TB):
        last = nc.vector.tensor_tensor(eq[:, t], eq[:, t], lower[:], ALU.mult)
    link(last)
    link(nc.vector.tensor_tensor(cmp[:], cmp[:], eq[:], ALU.add))
    link(nc.vector.tensor_reduce(rank[:], cmp[:], AX_X, ALU.add))



def moe_top1(nc, A, G):
    E, F = 4, 1024
    MF = F // P
    with ExitStack() as ctx:
        sb = lambda n, s, d=F32: ctx.enter_context(nc.sbuf_tensor("m0_" + n, s, d))
        psum = lambda n, s, d=F32: ctx.enter_context(nc.psum_tensor("m0_" + n, s, d))
        sem = ctx.enter_context(stage_semaphores(nc, "m0_"))
        f = front_buffers(nc, ctx, "m0_")
        wr = sb("wr", [P, KD, E])
        w1 = sb("w1", [P, KD, E, F])
        b1 = sb("b1", [E, F])
        wo = sb("wo", [P, MF, D])
        bo, gamma, beta = sb("bo", [P, D]), sb("gamma", [P, D]), sb("beta", [P, D])
        lower = sb("lower", [P, E, E])
        pick = sb("pick", [E, E, P])
        logits = sb("logits", [P, TB, E])
        cmp, eq = sb("cmp", [P, TB, E, E]), sb("eq", [P, TB, E, E])
        rank, onehot = sb("rank", [P, TB, E]), sb("onehot", [P, TB, E])
        onehotT = sb("onehotT", [E, S])
        xe = sb("xe", [P, E, KD, S])
        hT = sb("hT", [P, MF, S])
        y = sb("y", [P, TB, D])
        psT = psum("psT", [P, KD, S])
        psG = psum("psG", [P, S])
        psE = psum("psE", [P, S])
        psH = psum("psH", [P, 2, S])
        psY = psum("psY", [P, 2, S])
        loaded, consts_set = sem("loaded"), sem("consts_set")
        logits_ready, onehot_ready = sem("logits_ready"), sem("onehot_ready")
        onehotT_in_psum, onehotT_ready = sem("onehotT_in_psum"), sem("onehotT_ready")
        spread, xe_ready = sem("spread"), sem("xe_ready")
        h_in_psum, hT_ready = sem("h_in_psum"), sem("hT_ready")
        y_in_psum, y_taken = sem("y_in_psum"), sem("y_taken")
        chain = sem("chain")
        sems = [*f.sems, logits_ready, onehot_ready, onehotT_in_psum, onehotT_ready, spread, xe_ready,
                h_in_psum, hT_ready, y_in_psum, y_taken, chain]

        loads = [(wr[:], A["L0_ffn_W_router"].rearrange("(k p) e -> p k e", p=P)), (b1[:], A["L0_ffn_b1"]),
                 (wo[:], A["L0_ffn_Wo"].rearrange("(m p) d -> p m d", p=P)), (bo[:], bcast_row(A["L0_ffn_bo"])),
                 (gamma[:], bcast_row(A["L0_ffn_ln_gamma"])), (beta[:], bcast_row(A["L0_ffn_ln_beta"]))]
        loads += [(w1[:, k], A["L0_ffn_W1"][:, k * P:(k + 1) * P, :].rearrange("e p h -> p e h")) for k in range(KD)]
        load_weights(nc, loads, loaded)
        lower_triangle(nc, lower, E, consts_set)
        with nc.Block() as block:
            @block.gpsimd
            def _(pool):
                nc.gpsimd.memset(pick[:], 0.0).then_inc(consts_set, 1)
                pool.wait_ge(consts_set, 3)
                nc.gpsimd.affine_select(out=pick[:], in_=pick[:], compare_op=ALU.not_equal, fill=1.0, base=0,
                                        pattern=[[-1, E], [0, P]], channel_multiplier=1).then_inc(consts_set, 1)
                pool.wait_ge(consts_set, 4)

        def body(block, b):
            tile = lambda t: G.X[:, b * TB + t, :]

            @block.tensor
            def _(pe):
                transpose_tokens(nc, pe, f.xn, psT, G.ident, f.xn_ready, 0, f.xT_in_psum)
                pe.wait_ge(f.xT_ready, 1)
                for t in range(TB):
                    for k in range(KD):
                        last = nc.tensor.matmul(psG[:, t * E:(t + 1) * E], f.xT[:, k, t * P:(t + 1) * P], wr[:, k, :],
                                                start=(k == 0), stop=(k == KD - 1))
                last.then_inc(logits_ready, 1)
                pe.wait_ge(onehot_ready, 1)
                for t in range(TB):
                    last = nc.tensor.transpose(psG[0:E, t * P:(t + 1) * P], onehot[:, t, :], G.ident[:])
                last.then_inc(onehotT_in_psum, 1)
                pe.wait_ge(onehotT_ready, 1)
                for e in range(E):
                    out = psE[:] if e % 2 else psG[:]
                    if e >= 2:
                        pe.wait_ge(xe_ready, e - 1)
                    nc.tensor.matmul(out, pick[:, e, :], onehotT[:], start=True, stop=True).then_inc(spread, 1)
                for m in range(MF):
                    if m >= 2:
                        pe.wait_ge(hT_ready, m - 1)
                    cols = slice(m * P, (m + 1) * P)
                    nc.tensor.matmul(psH[:, m % 2, :], b1[:, cols], onehotT[:], start=True, stop=False)
                    for e in range(E):
                        if m == 0:
                            pe.wait_ge(xe_ready, e + 1)
                        for k in range(KD):
                            last = nc.tensor.matmul(psH[:, m % 2, :], w1[:, k, e, cols], xe[:, e, k, :],
                                                    start=False, stop=(e == E - 1 and k == KD - 1))
                    last.then_inc(h_in_psum, 1)
                for t in range(TB):
                    if t >= 2:
                        pe.wait_ge(y_taken, t - 1)
                    for m in range(MF):
                        if t == 0:
                            pe.wait_ge(hT_ready, m + 1)
                        last = nc.tensor.matmul(psY[:, t % 2, 0:D], hT[:, m, t * P:(t + 1) * P], wo[:, m, :],
                                                start=(m == 0), stop=(m == MF - 1))
                    last.then_inc(y_in_psum, 1)

            @block.scalar
            def _(act):
                ln_roots(nc, act, f)
                act.wait_ge(f.xT_in_psum, 1)
                nc.scalar.copy(f.xT[:], psT[:]).then_inc(f.xT_ready, 1)
                act.wait_ge(onehotT_in_psum, 1)
                nc.scalar.copy(onehotT[:], psG[0:E, :]).then_inc(onehotT_ready, 1)
                for m in range(MF):
                    act.wait_ge(h_in_psum, m + 1)
                    nc.scalar.activation(hT[:, m, :], psH[:, m % 2, :], ACT.Gelu).then_inc(hT_ready, 1)
                ln_roots(nc, act, f, done=2)

            @block.vector
            def _(dve):
                link = chained(dve, chain)
                ln_stats(nc, link, f, tile, LN_EPS)
                ln_apply(nc, dve, link, f, tile)
                dve.wait_ge(logits_ready, 1)
                link(nc.vector.tensor_copy(logits[:], psG[:, 0:TB * E].rearrange("p (t e) -> p t e", e=E)))
                rank_experts(nc, link, logits, rank, cmp, eq, lower, E)
                nc.vector.tensor_scalar(onehot[:], rank[:], 1.0, None, ALU.is_lt).then_inc(onehot_ready, 1)
                for e in range(E):
                    dve.wait_ge(spread, e + 1)
                    chosen = psE[:] if e % 2 else psG[:]
                    nc.vector.tensor_tensor(xe[:, e, 0, :], f.xT[:, 0, :], chosen, ALU.mult)
                    nc.vector.tensor_tensor(xe[:, e, 1, :], f.xT[:, 1, :], chosen, ALU.mult).then_inc(xe_ready, 1)
                for t in range(TB):
                    last = nc.vector.tensor_tensor(y[:, t, :], f.xn[:, t, :], bo[:], ALU.add)
                link(last)
                for t in range(TB):
                    dve.wait_ge(y_in_psum, t + 1)
                    nc.vector.tensor_tensor(y[:, t, :], y[:, t, :], psY[:, t % 2, 0:D], ALU.add).then_inc(y_taken, 1)
                dve.wait_ge(y_taken, TB)
                ln_stats(nc, link, f, lambda t: y[:, t, :], 1e-12)
                dve.wait_ge(f.std_ready, 2)
                link(nc.vector.reciprocal(f.rstd[:], f.std[:]))
                for t in range(TB):
                    last = nc.vector.tensor_scalar(y[:, t, :], y[:, t, :], f.meanvar[:, t, 0:1], f.rstd[:, t:t + 1],
                                                   ALU.subtract, ALU.mult)
                link(last)
                for t in range(TB):
                    last = nc.vector.tensor_tensor(y[:, t, :], y[:, t, :], gamma[:], ALU.mult)
                link(last)
                for t in range(TB):
                    last = nc.vector.tensor_tensor(tile(t), tile(t), beta[:], ALU.add)
                link(last)
                for t in range(TB):
                    last = nc.vector.tensor_tensor(tile(t), tile(t), y[:, t, :], ALU.add)
                link(last)

        batch_loop(nc, B, sems, body)



def pwl_ffn(nc, A, G):
    F = 1024
    MF = F // P
    Q = 256.0
    KNOT = 0.25
    STEPS = Q * KNOT
    with ExitStack() as ctx:
        sb = lambda n, s, d=F32: ctx.enter_context(nc.sbuf_tensor("p2_" + n, s, d))
        psum = lambda n, s, d=F32: ctx.enter_context(nc.psum_tensor("p2_" + n, s, d))
        sem = ctx.enter_context(stage_semaphores(nc, "p2_"))
        f = front_buffers(nc, ctx, "p2_")
        w1, w2 = sb("w1", [P, KD, F]), sb("w2", [P, MF, D])
        b1, b1q, b2 = sb("b1", [P, MF]), sb("b1q", [P, MF]), sb("b2", [P, D])
        half_knot, knot = sb("half_knot", [P, 1]), sb("knot", [P, 1])
        ring = 2
        v, u, c, fl = sb("v", [P, ring, S]), sb("u", [P, ring, S]), sb("c", [P, ring, S]), sb("fl", [P, ring, S])
        g0, g1, fr = sb("g0", [P, ring, S]), sb("g1", [P, ring, S]), sb("fr", [P, ring, S])
        hT = sb("hT", [P, MF, S])
        y = sb("y", [P, TB, D])
        psT = psum("psT", [P, KD, S])
        psH = psum("psH", [P, 3, S])
        psY = psum("psY", [P, 2, S])
        loaded, consts_set = sem("loaded"), sem("consts_set")
        h_in_psum, v_ready, u_ready, c_ready = sem("h_in_psum"), sem("v_ready"), sem("u_ready"), sem("c_ready")
        fl_ready, g_ready, hT_ready = sem("fl_ready"), sem("g_ready"), sem("hT_ready")
        y_in_psum, y_taken = sem("y_in_psum"), sem("y_taken")
        chain = sem("chain")
        sems = [*f.sems, h_in_psum, v_ready, u_ready, c_ready, fl_ready, g_ready, hT_ready, y_in_psum, y_taken, chain]
        load_weights(nc, [(w1[:], A["L2_ffn_w1"].rearrange("(k p) f -> p k f", p=P)),
                          (w2[:], A["L2_ffn_w2"].rearrange("(m p) d -> p m d", p=P)),
                          (b1[:], A["L2_ffn_b1"]),
                          (b2[:], bcast_row(A["L2_ffn_b2"]))], loaded)
        with nc.Block() as block:
            @block.vector
            def _(dve):
                nc.vector.tensor_scalar(b1q[:], b1[:], Q, None, ALU.mult).then_inc(consts_set, 1)
                nc.vector.memset(half_knot[:], -(STEPS / 2 - 0.5) / STEPS).then_inc(consts_set, 1)
                nc.vector.memset(knot[:], KNOT).then_inc(consts_set, 1)
                dve.wait_ge(consts_set, 3)

        def body(block, b):
            tile = lambda t: G.X[:, b * TB + t, :]

            @block.tensor
            def _(pe):
                transpose_tokens(nc, pe, f.xn, psT, G.ident, f.xn_ready, 0, f.xT_in_psum)
                pe.wait_ge(f.xT_ready, 1)
                for m in range(MF):
                    if m >= 3:
                        pe.wait_ge(v_ready, m - 2)
                    for k in range(KD):
                        last = nc.tensor.matmul(psH[:, m % 3, :], w1[:, k, m * P:(m + 1) * P], f.xT[:, k, :],
                                                start=(k == 0), stop=(k == KD - 1))
                    last.then_inc(h_in_psum, 1)
                for t in range(TB):
                    if t >= 2:
                        pe.wait_ge(y_taken, t - 1)
                    for m in range(MF):
                        if t == 0:
                            pe.wait_ge(hT_ready, m + 1)
                        last = nc.tensor.matmul(psY[:, t % 2, 0:D], hT[:, m, t * P:(t + 1) * P], w2[:, m, :],
                                                start=(m == 0), stop=(m == MF - 1))
                    last.then_inc(y_in_psum, 1)

            @block.scalar
            def _(act):
                ln_roots(nc, act, f)
                act.wait_ge(f.xT_in_psum, 1)
                nc.scalar.copy(f.xT[:], psT[:]).then_inc(f.xT_ready, 1)

                def scaled(m):
                    act.wait_ge(h_in_psum, m + 1)
                    if m >= ring:
                        act.wait_ge(u_ready, m - ring + 1)
                    nc.scalar.activation(v[:, m % ring, :], psH[:, m % 3, :], ACT.Identity, bias=b1q[:, m:m + 1],
                                         scale=Q).then_inc(v_ready, 1)

                scaled(0)
                for m in range(MF):
                    act.wait_ge(u_ready, m + 1)
                    nc.scalar.activation(c[:, m % ring, :], u[:, m % ring, :], ACT.Identity, bias=half_knot[:],
                                         scale=1.0 / STEPS).then_inc(c_ready, 1)
                    if m + 1 < MF:
                        scaled(m + 1)
                    act.wait_ge(fl_ready, m + 1)
                    if m >= ring:
                        act.wait_ge(hT_ready, m - ring + 1)
                    nc.scalar.activation(g0[:, m % ring, :], fl[:, m % ring, :], ACT.Gelu, scale=KNOT)
                    nc.scalar.activation(g1[:, m % ring, :], fl[:, m % ring, :], ACT.Gelu, scale=KNOT,
                                         bias=knot[:]).then_inc(g_ready, 1)

            @block.vector
            def _(dve):
                link = chained(dve, chain)
                ln_stats(nc, link, f, tile, LN_EPS)
                ln_apply(nc, dve, link, f, tile)

                def steps(m):
                    dve.wait_ge(v_ready, m + 1)
                    nc.vector.tensor_scalar(u[:, m % ring, :], v[:, m % ring, :], ROUNDER, ROUNDER, ALU.add,
                                            ALU.subtract).then_inc(u_ready, 1)

                steps(0)
                for m in range(MF):
                    r = m % ring
                    dve.wait_ge(c_ready, m + 1)
                    nc.vector.tensor_scalar(fl[:, r, :], c[:, r, :], ROUNDER, ROUNDER, ALU.add,
                                            ALU.subtract).then_inc(fl_ready, 1)
                    dve.wait_ge(fl_ready, m + 1)
                    link(nc.vector.scalar_tensor_tensor(fr[:, r, :], u[:, r, :], 1.0 / STEPS, fl[:, r, :],
                                                        ALU.mult, ALU.subtract))
                    if m + 1 < MF:
                        steps(m + 1)
                    dve.wait_ge(g_ready, m + 1)
                    link(nc.vector.tensor_tensor(g1[:, r, :], g1[:, r, :], g0[:, r, :], ALU.subtract))
                    link(nc.vector.tensor_tensor(g1[:, r, :], g1[:, r, :], fr[:, r, :], ALU.mult))
                    link(nc.vector.tensor_tensor(g1[:, r, :], g1[:, r, :], g0[:, r, :], ALU.add))
                    link(nc.vector.tensor_scalar(g1[:, r, :], g1[:, r, :], Q, ROUNDER, ALU.mult, ALU.add))
                    nc.vector.tensor_scalar(hT[:, m, :], g1[:, r, :], ROUNDER, 1.0 / Q, ALU.subtract,
                                            ALU.mult).then_inc(hT_ready, 1)
                for t in range(TB):
                    dve.wait_ge(y_in_psum, t + 1)
                    nc.vector.tensor_tensor(y[:, t, :], psY[:, t % 2, 0:D], b2[:], ALU.add).then_inc(y_taken, 1)
                dve.wait_ge(y_taken, TB)
                link(nc.vector.tensor_scalar(y[:], y[:], Q, ROUNDER, ALU.mult, ALU.add))
                link(nc.vector.tensor_scalar(y[:], y[:], ROUNDER, 1.0 / Q, ALU.subtract, ALU.mult))
                for t in range(TB):
                    last = nc.vector.tensor_tensor(tile(t), tile(t), y[:, t, :], ALU.add)
                link(last)

        batch_loop(nc, B, sems, body)



H = 16
DH = D // H
VW = DH + 1
GH = 4
NG = H // GH
HIDDEN = -1e30
Q_PARTS = (0, 0, 1, 1, 0, 2)
K_PARTS = (0, 1, 0, 1, 2, 0)
STACK = len(Q_PARTS) * DH


def split_parts(nc, link, src, parts, rest):
    link(nc.vector.tensor_copy(parts[0], src))
    link(nc.vector.tensor_tensor(rest, src, parts[0], ALU.subtract))
    link(nc.vector.tensor_copy(parts[1], rest))
    return nc.vector.tensor_tensor(parts[2], rest, parts[1], ALU.subtract)


def attention_projections(nc, A, G, nm, V, q_dram, k_dram, w, q_scale):
    with ExitStack() as ctx:
        sb = lambda n, s, d=F32: ctx.enter_context(nc.sbuf_tensor(nm + n, s, d))
        psum = lambda n, s, d=F32: ctx.enter_context(nc.psum_tensor(nm + n, s, d))
        sem = ctx.enter_context(stage_semaphores(nc, nm))
        f = front_buffers(nc, ctx, nm)
        wq, wk, wv = (sb(n, [P, KD, D]) for n in ("wq", "wk", "wv"))
        bq, bqs, bk, bv = sb("bq", [P, KD]), sb("bqs", [P, KD]), sb("bk", [P, KD]), sb("bv", [P, D])
        cT = sb("cT", [P, KD, S])
        qf, kf, rest = sb("qf", [P, KD, S]), sb("kf", [P, KD, S]), sb("rest", [P, KD, S])
        qp, kp = sb("qp", [P, 3, KD, S], BF16), sb("kp", [P, 3, KD, S], BF16)
        psT, psK, psV = psum("psT", [P, KD, S]), psum("psK", [P, KD, S]), psum("psV", [P, 2, S])
        psQ = psum("psQ", [P, KD, S])
        loaded, set_up = sem("loaded"), sem("set_up")
        ctx_loaded, q_in_psum, k_in_psum, v_in_psum = (sem(n) for n in ("ctx_loaded", "q_in_psum", "k_in_psum", "v_in_psum"))
        q_ready, k_ready, v_taken, qp_ready, kp_ready = (sem(n) for n in ("q_ready", "k_ready", "v_taken", "qp_ready", "kp_ready"))
        parts_stored, chain = sem("parts_stored"), sem("chain")
        sems = [*f.sems, ctx_loaded, q_in_psum, k_in_psum, v_in_psum, q_ready, k_ready, v_taken, qp_ready,
                kp_ready, parts_stored, chain]
        rows = lambda x: x.rearrange("(k p) d -> p k d", p=P)
        load_weights(nc, [(wq[:], rows(w.Wq)), (wk[:], rows(w.Wk)), (wv[:], rows(w.Wv)), (bq[:], w.bq), (bk[:], w.bk),
                          (bv[:], bcast_row(w.bv))], loaded)
        with nc.Block() as block:
            @block.vector
            def _(dve):
                nc.vector.tensor_scalar(bqs[:], bq[:], q_scale, None, ALU.mult).then_inc(set_up, 1)
                nc.vector.memset(V[:, :, :, DH:VW], 1.0).then_inc(set_up, 1)
                dve.wait_ge(set_up, 2)
        ctxT = A["ctxT"].rearrange("(k p) t -> p k t", p=P)

        def body(block, b):
            tile = lambda t: G.X[:, b * TB + t, :]
            cols = bass.ds(b * S, S)

            @block.sync
            def _(sp):
                sp.dma_start(cT[:], ctxT[:, :, cols]).then_inc(ctx_loaded, 16)
                for ready, parts, dram in ((kp_ready, kp, k_dram), (qp_ready, qp, q_dram)):
                    sp.wait_ge(ready, 1)
                    for i in range(3):
                        sp.dma_start(dram[i].rearrange("(k p) t -> p k t", p=P)[:, :, cols],
                                     parts[:, i]).then_inc(parts_stored, 16)
                sp.wait_ge(parts_stored, 6 * 16)

            @block.tensor
            def _(pe):
                pe.wait_ge(ctx_loaded, 16)
                for m in range(KD):
                    for k in range(KD):
                        last = nc.tensor.matmul(psK[:, m, :], wk[:, k, m * P:(m + 1) * P], cT[:, k, :],
                                                start=(k == 0), stop=(k == KD - 1))
                last.then_inc(k_in_psum, 1)
                for t in range(TB):
                    if t >= 2:
                        pe.wait_ge(v_taken, t - 1)
                    for k in range(KD):
                        last = nc.tensor.matmul(psV[:, t % 2, 0:D], cT[:, k, t * P:(t + 1) * P], wv[:, k, :],
                                                start=(k == 0), stop=(k == KD - 1))
                    last.then_inc(v_in_psum, 1)
                transpose_tokens(nc, pe, f.xn, psT, G.ident, f.xn_ready, 0, f.xT_in_psum)
                pe.wait_ge(f.xT_ready, 1)
                for m in range(KD):
                    for k in range(KD):
                        last = nc.tensor.matmul(psQ[:, m, :], wq[:, k, m * P:(m + 1) * P], f.xT[:, k, :],
                                                start=(k == 0), stop=(k == KD - 1))
                last.then_inc(q_in_psum, 1)

            @block.scalar
            def _(act):
                ln_roots(nc, act, f)
                act.wait_ge(k_in_psum, 1)
                for m in range(KD):
                    last = nc.scalar.activation(kf[:, m, :], psK[:, m, :], ACT.Identity, bias=bk[:, m:m + 1], scale=1.0)
                last.then_inc(k_ready, 1)
                act.wait_ge(f.xT_in_psum, 1)
                nc.scalar.copy(f.xT[:], psT[:]).then_inc(f.xT_ready, 1)
                act.wait_ge(q_in_psum, 1)
                for m in range(KD):
                    last = nc.scalar.activation(qf[:, m, :], psQ[:, m, :], ACT.Identity, bias=bqs[:, m:m + 1], scale=q_scale)
                last.then_inc(q_ready, 1)

            @block.vector
            def _(dve):
                link = chained(dve, chain)
                ln_stats(nc, link, f, tile, LN_EPS)
                ln_apply(nc, dve, link, f, tile)
                for t in range(TB):
                    dve.wait_ge(v_in_psum, t + 1)
                    nc.vector.tensor_tensor(V[:, b * TB + t, :, 0:DH], psV[:, t % 2, 0:D].rearrange("p (h d) -> p h d", h=H),
                                            bv[:].rearrange("p (h d) -> p h d", h=H), ALU.add).then_inc(v_taken, 1)
                for ready, x, parts, done in ((k_ready, kf, kp, kp_ready), (q_ready, qf, qp, qp_ready)):
                    dve.wait_ge(ready, 1)
                    split_parts(nc, link, x[:], [parts[:, i] for i in range(3)], rest[:]).then_inc(done, 1)
                    dve.wait_ge(done, 1)

        batch_loop(nc, B, sems, body)


def attention(nc, A, G, nm, w, q_scale, hidden=None, added=None):
    mask_row = STACK
    max_row = STACK + (3 if added is not None else 0)
    ROWS = max_row + 3
    LAG = 7
    NSTEP = H + LAG + 1
    with ExitStack() as outer:
        V = outer.enter_context(nc.sbuf_tensor(nm + "V", [P, NT, H, VW], F32))
        q_dram = nc.dram_tensor(nm + "q_parts", [3, D, N_TOK], BF16).ap()
        k_dram = nc.dram_tensor(nm + "k_parts", [3, D, N_TOK], BF16).ap()
        added_dram = nc.dram_tensor(nm + "added_parts", [3, N_TOK], BF16).ap()
        attention_projections(nc, A, G, nm + "p_", V, q_dram, k_dram, w, q_scale)
        ctx = outer
        sb = lambda n, s, d=F32: ctx.enter_context(nc.sbuf_tensor(nm + n, s, d))
        psum = lambda n, s, d=F32: ctx.enter_context(nc.psum_tensor(nm + n, s, d))
        sem = ctx.enter_context(stage_semaphores(nc, nm))
        wo, bo = sb("wo", [P, KD, D]), sb("bo", [P, D])
        qs, ks = sb("qs", [P, H, S], BF16), sb("ks", [P, H, S], BF16)
        mx = sb("mx", [P, NG, GH, TB])
        nmx, nrest = sb("nmx", [P, TB, GH]), sb("nrest", [P, TB, GH])
        nparts = sb("nparts", [P, TB, 3, GH], BF16)
        npartsT = sb("npartsT", [3 * GH, S], BF16)
        pT = sb("pT", [P, 2, TB, S])
        rden, oraw, on = sb("rden", [P, TB, GH]), sb("oraw", [P, TB, GH, VW]), sb("on", [P, TB, D])
        oT = sb("oT", [P, KD, S])
        psA = psum("psA", [P, 2, S])
        psS = psum("psS", [P, 2, 2, S])
        psO = psum("psO", [P, TB, GH, VW])
        psN = psum("psN", [P, S], BF16)
        loaded, set_up = sem("loaded"), sem("set_up")
        group_loaded = [sem(f"group_loaded{g}") for g in range(NG)]
        a_ready, a_used, max_ready, max_turned, max_copied = (sem(n) for n in ("a_ready", "a_used", "max_ready", "max_turned", "max_copied"))
        max_stored = [sem(f"max_stored{g}") for g in range(NG)]
        s_ready, exp_done, pv_done, o_taken = (sem(n) for n in ("s_ready", "exp_done", "pv_done", "o_taken"))
        head_done = sem("head_done")
        on_ready, oT_in_psum, oT_ready, y_ready, y_taken, chain = (sem(n) for n in ("on_ready", "oT_in_psum", "oT_ready", "y_ready", "y_taken", "chain"))
        u_in_psum, u_ready, e0_ready = sem("u_in_psum"), sem("u_ready"), sem("e0_ready")
        mask_loaded, maskT_loaded, mask_done = sem("mask_loaded"), sem("maskT_loaded"), sem("mask_done")
        sems = [*group_loaded, a_ready, a_used, max_ready, max_turned, max_copied, *max_stored, s_ready, exp_done,
                pv_done, o_taken, head_done, on_ready, oT_in_psum, oT_ready, y_ready, y_taken, chain, u_in_psum,
                u_ready, e0_ready, mask_loaded, maskT_loaded, mask_done]
        load_weights(nc, [(wo[:], w.Wo.rearrange("(k p) d -> p k d", p=P)), (bo[:], bcast_row(w.bo))], loaded)

        def load_group(sp, g, b):
            heads = slice(g * GH, (g + 1) * GH)
            n = 0
            for stack, dram, which in ((qs, q_dram, Q_PARTS), (ks, k_dram, K_PARTS)):
                for r, part in enumerate(which):
                    src = dram[part, g * GH * DH:(g + 1) * GH * DH, :].rearrange("(h d) t -> d h t", d=DH)
                    sp.dma_start(stack[r * DH:(r + 1) * DH, heads, :], src[:, :, bass.ds(b * S, S)]).then_inc(group_loaded[g], 16)
                    n += 1
            if added is not None:
                src = added_dram[:, bass.ds(b * S, S)].unsqueeze(1).to_broadcast([3, GH, S])
                sp.dma_start(ks[mask_row:mask_row + 3, heads, :], src).then_inc(group_loaded[g], 16)
                n += 1
            return n

        if added is not None:
            madd, mparts, mrest = sb("madd", [B, S]), sb("mparts", [B, 3, S], BF16), sb("mrest", [B, S])
            with nc.Block() as block:
                @block.sync
                def _(sp):
                    sp.dma_start(madd[:], added.rearrange("b x y s -> b (x y s)")).then_inc(loaded, 16)
                    sp.wait_ge(set_up, 1)
                    for i in range(3):
                        sp.dma_start(added_dram[i].rearrange("(b s) -> b s", b=B), mparts[:, i, :]).then_inc(loaded, 16)
                    sp.wait_ge(loaded, 16 * 6)

                @block.vector
                def _(dve):
                    link = chained(dve, chain)
                    dve.wait_ge(loaded, 16 * 3)
                    split_parts(nc, link, madd[:], [mparts[:, i, :] for i in range(3)], mrest[:]).then_inc(set_up, 1)
            nc.sync.sem_clear(chain)
            nc.all_engine_barrier()

        if hidden is not None:
            mask, maskT, score = hidden
            score = float(score)
            m_int = sb("m_int", [P, TB, S], I32)
            hide_q, hide_k = sb("hide_q", [P, TB, S], BF16), sb("hide_k", [P, TB, S], BF16)
            is_hidden = sb("is_hidden", [P, TB, S])
            floor_ = sb("floor", [P, TB])
            usum, e0 = sb("usum", [P, TB, H, VW]), sb("e0", [P, NG, GH, TB])
            scored = sb("scored", [P, S])
            score_bias = sb("score_bias", [P, 1])

            def load_mask(sp, which, b, done):
                sp.dma_start(m_int[:], which[b] if isinstance(b, int) else
                             which[bass.ds(b, 1)].rearrange("a p t s -> p (a t) s")).then_inc(done, 16)

            mask4 = mask.rearrange("b x (t p) s -> b p (x t) s", p=P)
            maskT4 = maskT.rearrange("b (t p) s -> b p t s", p=P)

            def mask_by_query(link):
                link(nc.vector.tensor_scalar(hide_q[:], m_int[:], 0.0, HIDDEN, ALU.is_equal, ALU.mult))
                link(nc.vector.tensor_reduce(floor_[:], hide_q[:], AX_X, ALU.min))
                link(nc.vector.tensor_scalar(floor_[:], floor_[:], 0.0, HIDDEN, ALU.is_equal, ALU.mult))
                return nc.vector.tensor_scalar(floor_[:], floor_[:], score, None, ALU.add)

            def mask_by_key(link):
                link(nc.vector.tensor_scalar(is_hidden[:], m_int[:], 0.0, None, ALU.is_equal))
                return nc.vector.tensor_scalar(hide_k[:], is_hidden[:], HIDDEN, None, ALU.mult)

        with nc.Block() as block:
            @block.sync
            def _(sp):
                sp.wait_ge(set_up, 2 if added is None else 3)
                for g in range(NG):
                    n = load_group(sp, g, 0)
                for g in range(NG):
                    sp.wait_ge(group_loaded[g], 16 * n)
                if hidden is not None:
                    load_mask(sp, mask4, 0, mask_loaded)
                    sp.wait_ge(mask_done, 1)
                    load_mask(sp, maskT4, 0, maskT_loaded)

            @block.vector
            def _(dve):
                nc.vector.memset(qs[STACK:P], 1.0).then_inc(set_up, 1)
                nc.vector.memset(ks[STACK:P], 1.0).then_inc(set_up, 1)
                if hidden is not None:
                    link = chained(dve, chain)
                    nc.vector.memset(score_bias[:], score)
                    dve.wait_ge(mask_loaded, 16)
                    mask_by_query(link).then_inc(mask_done, 1)
                    dve.wait_ge(maskT_loaded, 16)
                    link(mask_by_key(link))
        for s in (chain, mask_loaded, maskT_loaded, mask_done, *group_loaded):
            nc.sync.sem_clear(s)
        nc.all_engine_barrier()

        def body(block, b):
            nxt = (b + 1) % B

            @block.sync
            def _(sp):
                for g in range(NG):
                    sp.wait_ge(max_copied, g + 1)
                    for i in range(3):
                        row = max_row + i
                        sp.dma_start(qs[row:row + 1, g * GH:(g + 1) * GH, :],
                                     npartsT[i * GH:(i + 1) * GH, :]).then_inc(max_stored[g], 16)
                if hidden is not None:
                    load_mask(sp, mask4, nxt, mask_loaded)
                for g in range(NG):
                    sp.wait_ge(head_done, (g + 1) * GH)
                    n = load_group(sp, g, nxt)
                    if hidden is not None and g == NG - 1:
                        sp.wait_ge(mask_done, 1)
                        load_mask(sp, maskT4, nxt, maskT_loaded)
                for g in range(NG):
                    sp.wait_ge(group_loaded[g], 16 * n)

            @block.tensor
            def _(pe):
                def maxima_scores(h, q):
                    n = h * TB + q
                    if n >= 2:
                        pe.wait_ge(a_used, n - 1)
                    nc.tensor.matmul(psA[:, n % 2, :], qs[0:max_row, h, q * P:(q + 1) * P], ks[0:max_row, h, :],
                                     start=True, stop=True).then_inc(a_ready, 1)

                def exp_scores(h, u):
                    n = 2 * h + u
                    if u == 0 and h % GH == 0:
                        pe.wait_ge(max_stored[h // GH], 3 * 16)
                    if n >= 2:
                        pe.wait_ge(exp_done, n - 1)
                    elif hidden is not None:
                        pe.wait_ge(u_ready, 4)
                    for j in range(2):
                        kt = 2 * u + j
                        if hidden is not None:
                            nc.tensor.matmul(psS[:, n % 2, j, :], G.identb[:], hide_k[:, kt, :], start=True, stop=False)
                        last = nc.tensor.matmul(psS[:, n % 2, j, :], ks[0:ROWS, h, kt * P:(kt + 1) * P], qs[0:ROWS, h, :],
                                                start=(hidden is None), stop=True)
                    last.then_inc(s_ready, 1)

                def values(h, qs_):
                    g, j = h // GH, h % GH
                    for q in qs_:
                        if q == 0:
                            pe.wait_ge(exp_done, 2 * h + 2)
                            if j == 0 and g > 0:
                                pe.wait_ge(o_taken, g)
                        for kt in range(TB):
                            last = nc.tensor.matmul(psO[:, q, j, :], pT[:, h % 2, kt, q * P:(q + 1) * P],
                                                    V[:, b * TB + kt, h, :], start=(kt == 0), stop=(kt == TB - 1))
                    if qs_[-1] == TB - 1:
                        last.then_inc(pv_done, 1)

                if hidden is not None:
                    for q in range(TB):
                        for kt in range(TB):
                            last = nc.tensor.matmul(psS[:, q // 2, q % 2, 0:H * VW], is_hidden[:, kt, q * P:(q + 1) * P],
                                                    V[:, b * TB + kt, :, :], start=(kt == 0), stop=(kt == TB - 1))
                        last.then_inc(u_in_psum, 1)
                for i in range(NSTEP):
                    h, hv = i - LAG, i - LAG - 1
                    for half in range(2):
                        if i < H:
                            maxima_scores(i, 2 * half)
                            maxima_scores(i, 2 * half + 1)
                        if 0 <= h < H:
                            exp_scores(h, half)
                        if 0 <= hv < H:
                            values(hv, (2 * half, 2 * half + 1))
                    if i % GH == 0 and i // GH in range(1, NG + 1):
                        g = i // GH - 1
                        pe.wait_ge(max_ready, g + 1)
                        if g > 0:
                            pe.wait_ge(max_copied, g)
                        for q in range(TB):
                            last = nc.tensor.transpose(psN[0:3 * GH, q * P:(q + 1) * P], nparts[:, q, :, :], G.identb[:])
                        last.then_inc(max_turned, 1)
                pe.wait_ge(on_ready, NG)
                pe.wait_ge(exp_done, 2 * H)
                for q in range(TB):
                    for k in range(KD):
                        last = nc.tensor.transpose(psS[:, 0, k, q * P:(q + 1) * P], on[:, q, k * P:(k + 1) * P], G.ident[:])
                last.then_inc(oT_in_psum, 1)
                pe.wait_ge(oT_ready, 1)
                for q in range(TB):
                    if q >= 2:
                        pe.wait_ge(y_taken, q - 1)
                    for k in range(KD):
                        last = nc.tensor.matmul(psA[:, q % 2, 0:D], oT[:, k, q * P:(q + 1) * P], wo[:, k, :],
                                                start=(k == 0), stop=(k == KD - 1))
                    last.then_inc(y_ready, 1)

            @block.scalar
            def _(act):
                if hidden is not None:
                    for q in range(TB):
                        act.wait_ge(u_in_psum, q + 1)
                        nc.scalar.copy(usum[:, q, :, :], psS[:, q // 2, q % 2, 0:H * VW].rearrange("p (h v) -> p h v", h=H)
                                       ).then_inc(u_ready, 1)
                for i in range(NSTEP):
                    if i % GH == 1 and 1 <= i // GH <= NG:
                        g = i // GH - 1
                        act.wait_ge(max_turned, g + 1)
                        if g > 0:
                            act.wait_ge(max_stored[g - 1], 3 * 16)
                        nc.scalar.copy(npartsT[:], psN[0:3 * GH, :]).then_inc(max_copied, 1)
                        if hidden is not None:
                            nc.scalar.activation(e0[:, g], mx[:, g], ACT.Exp, bias=score_bias[:], scale=-1.0).then_inc(e0_ready, 1)
                    h = i - LAG
                    if 0 <= h < H:
                        for u in range(2):
                            n = 2 * h + u
                            act.wait_ge(s_ready, n + 1)
                            if h >= 2 and u == 0:
                                act.wait_ge(pv_done, h - 1)
                            e = nc.scalar.activation(pT[:, h % 2, 2 * u:2 * u + 2, :], psS[:, n % 2], ACT.Exp)
                            e.then_inc(exp_done, 1)
                            if u == 1:
                                act.wait_ge(exp_done, n + 1)
                                act.sem_inc(head_done, 1)
                act.wait_ge(oT_in_psum, 1)
                nc.scalar.copy(oT[:], psS[:, 0]).then_inc(oT_ready, 1)

            @block.vector
            def _(dve):
                link = chained(dve, chain)

                def split_maxima(g):
                    m = mx[:, g].rearrange("p j q -> p q j")
                    if hidden is not None:
                        link(nc.vector.tensor_tensor(mx[:, g], mx[:, g], floor_[:].unsqueeze(1).to_broadcast([P, GH, TB]), ALU.max))
                    link(nc.vector.tensor_scalar(nmx[:], m, -1.0, None, ALU.mult))
                    if g > 0:
                        dve.wait_ge(max_turned, g)
                    split_parts(nc, link, nmx[:], [nparts[:, :, p_, :] for p_ in range(3)], nrest[:]).then_inc(max_ready, 1)

                def take_output(g):
                    heads = slice(g * GH, (g + 1) * GH)
                    dve.wait_ge(pv_done, (g + 1) * GH)
                    if hidden is not None:
                        dve.wait_ge(e0_ready, g + 1)
                        weight = e0[:, g].rearrange("p j q -> p q j").unsqueeze(3).to_broadcast([P, TB, GH, VW])
                        link(nc.vector.tensor_tensor(oraw[:], usum[:, :, heads, :], weight, ALU.mult))
                        link(nc.vector.tensor_tensor(oraw[:], oraw[:], psO[:], ALU.add))
                        src = oraw
                    else:
                        link(nc.vector.tensor_copy(oraw[:], psO[:]))
                    dve.sem_inc(o_taken, 1)
                    link(nc.vector.reciprocal(rden[:], oraw[:, :, :, DH]))
                    nc.vector.tensor_tensor(on[:].rearrange("p q (h d) -> p q h d", h=H)[:, :, heads, :], oraw[:, :, :, 0:DH],
                                            rden[:].unsqueeze(3).to_broadcast([P, TB, GH, DH]), ALU.mult).then_inc(on_ready, 1)
                    dve.wait_ge(on_ready, g + 1)

                for i in range(NSTEP + 1):
                    if i % GH == 0 and 1 <= i // GH <= NG:
                        split_maxima(i // GH - 1)
                    done = i - LAG - 2
                    if done >= 0 and done % GH == GH - 1:
                        take_output(done // GH)
                    if i < H:
                        for q in range(TB):
                            n = i * TB + q
                            dve.wait_ge(a_ready, n + 1)
                            out = mx[:, i // GH, i % GH, q:q + 1]
                            if hidden is not None:
                                if n > 0:
                                    dve.wait_ge(a_used, n)
                                nc.vector.tensor_tensor_reduce(out=scored[:], in0=psA[:, n % 2, :], in1=hide_q[:, q, :], scale=1.0,
                                                               scalar=HIDDEN, op0=ALU.add, op1=ALU.max, accum_out=out).then_inc(a_used, 1)
                            else:
                                nc.vector.tensor_reduce(out, psA[:, n % 2, :], AX_X, ALU.max).then_inc(a_used, 1)
                        if i % GH == GH - 1:
                            dve.wait_ge(a_used, (i + 1) * TB)
                    if hidden is not None and i == H + 1:
                        dve.wait_ge(mask_loaded, 16)
                        mask_by_query(link).then_inc(mask_done, 1)
                        dve.wait_ge(mask_done, 1)
                if hidden is not None:
                    dve.wait_ge(maskT_loaded, 16)
                    link(mask_by_key(link))
                for q in range(TB):
                    tile = G.X[:, b * TB + q, :]
                    link(nc.vector.tensor_tensor(tile, tile, bo[:], ALU.add))
                    dve.wait_ge(y_ready, q + 1)
                    nc.vector.tensor_tensor(tile, tile, psA[:, q % 2, 0:D], ALU.add).then_inc(y_taken, 1)
                dve.wait_ge(y_taken, TB)

        batch_loop(nc, B, sems, body)


class AttentionWeights:

    def __init__(self, Wq, Wk, Wv, Wo, bq, bk, bv, bo):
        self.Wq, self.Wk, self.Wv, self.Wo = Wq, Wk, Wv, Wo
        self.bq, self.bk, self.bv, self.bo = bq, bk, bv, bo


def attention0(nc, A, G):
    w = AttentionWeights(*(A["L0_xattn_" + n] for n in ("Wq", "Wk", "Wv", "Wo", "bq", "bk", "bv", "bo")))
    scale = 1.0 / D**0.5
    attention(nc, A, G, "a0_", w, scale, hidden=(A["mask_Bx1xSxS2_ik1"], A["maskT"], 1e-20 * scale))


def attention2(nc, A, G):
    w = AttentionWeights(*(A["L2_xattn_" + n] for n in ("Wq", "Wk", "Wv", "Wo", "bq", "bk", "bv", "bo")))
    attention(nc, A, G, "a2_", w, DH**-0.5)


def attention3(nc, A, G):
    kv = A["L3_xattn_Wkv"]
    w = AttentionWeights(Wq=A["L3_xattn_Wq"], Wk=kv[:, 0:D], Wv=kv[:, D:2 * D], Wo=A["L3_xattn_Wp"], bq=A["L3_xattn_bq"],
                        bk=A["L3_xattn_bk"], bv=A["L3_xattn_bkv"][D:2 * D], bo=A["L3_xattn_bp"])
    attention(nc, A, G, "a3_", w, DH**-0.5, added=A["mask_Bx1x1xS2_ff0"])



LH = 8
LD = 128
LW = LH * LD


def cosine_attention(nc, A, G):
    z_dram = nc.dram_tensor("l1_zT", [2, D, N_TOK], F32).ap()
    with ExitStack() as ctx:
        sb = lambda n, s, d=F32: ctx.enter_context(nc.sbuf_tensor("l1_" + n, s, d))
        sem = ctx.enter_context(stage_semaphores(nc, "l1_"))
        win, wout = sb("win", [P, KD, LW]), sb("wout", [P, LH, D])
        bout = sb("bout", [P, D])
        coef = sb("coef", [P, 2 * LH])
        wwh = sb("wwh", [LH, 1])
        gsum = sb("gsum", [P, KD, D + 2])
        loaded = sem("loaded")
        load_weights(nc, [(win[:], A["L1_xattn_w_in"].rearrange("(k p) o -> p k o", p=P)),
                          (wout[:], A["L1_xattn_w_out"].rearrange("(h p) d -> p h d", p=P)),
                          (bout[:], bcast_row(A["L1_xattn_b_out"]))], loaded)
        cosine_sums(nc, A, G, z_dram, gsum)
        cosine_weights(nc, A, G, win, gsum, coef, wwh)
        cosine_apply(nc, A, G, z_dram, win, wout, bout, coef, wwh)


def cosine_sums(nc, A, G, z_dram, gsum):
    with ExitStack() as ctx:
        sb = lambda n, s, d=F32: ctx.enter_context(nc.sbuf_tensor("l1s_" + n, s, d))
        psum = lambda n, s, d=F32: ctx.enter_context(nc.psum_tensor("l1s_" + n, s, d))
        sem = ctx.enter_context(stage_semaphores(nc, "l1s_"))
        f = front_buffers(nc, ctx, "l1s_")
        cx, zq, zk = sb("cx", [P, TB, D]), sb("zq", [P, TB, D]), sb("zk", [P, TB, D])
        lng, lnb, ones = sb("lng", [P, D]), sb("lnb", [P, D]), sb("ones", [P, 1])
        zT = sb("zT", [P, 2, KD, S])
        psT = psum("psT", [P, 2, KD, S])
        psG = psum("psG", [P, KD, S])
        loaded, set_up, cx_loaded = sem("loaded"), sem("set_up"), sem("cx_loaded")
        zq_ready, zk_ready, zT_in_psum, zT_ready = sem("zq_ready"), sem("zk_ready"), sem("zT_in_psum"), sem("zT_ready")
        sums_ready, z_stored, chain = sem("sums_ready"), sem("z_stored"), sem("chain")
        sems = [*f.sems, cx_loaded, zq_ready, zk_ready, zT_in_psum, zT_ready, sums_ready, z_stored, chain]
        load_weights(nc, [(lng[:], bcast_row(A["L1_xattn_ln_g"])), (lnb[:], bcast_row(A["L1_xattn_ln_b"]))], loaded)
        with nc.Block() as block:
            @block.vector
            def _(dve):
                nc.vector.memset(gsum[:], 0.0).then_inc(set_up, 1)
                nc.vector.memset(ones[:], 1.0).then_inc(set_up, 1)
                dve.wait_ge(set_up, 2)
        ctx_rows = A["ctx_1024"].rearrange("b (t p) d -> b p t d", p=P)

        def body(block, b):
            cols = bass.ds(b * S, S)

            @block.sync
            def _(sp):
                sp.dma_start(cx[:], ctx_rows[bass.ds(b, 1)].rearrange("a p t d -> p (a t) d")).then_inc(cx_loaded, 16)
                for i in range(2):
                    sp.wait_ge(zT_ready, i + 1)
                    sp.dma_start(z_dram[i].rearrange("(k p) t -> p k t", p=P)[:, :, cols], zT[:, i]).then_inc(z_stored, 16)
                sp.wait_ge(z_stored, 32)

            @block.tensor
            def _(pe):
                for i, (z, ready) in enumerate(((zk, zk_ready), (zq, zq_ready))):
                    pe.wait_ge(ready, 1)
                    for t in range(TB):
                        for k in range(KD):
                            last = nc.tensor.transpose(psT[:, i, k, t * P:(t + 1) * P], z[:, t, k * P:(k + 1) * P], G.ident[:])
                    last.then_inc(zT_in_psum, 1)
                for m in range(KD):
                    half = slice(m * P, (m + 1) * P)
                    for out, z, rhs in ((psG[:, m, 0:D], zq, lambda t: zq[:, t, :]), (psG[:, m, D:D + 1], zq, lambda t: ones[:]),
                                        (psG[:, m, D + 1:D + 2], zk, lambda t: ones[:])):
                        for t in range(TB):
                            last = nc.tensor.matmul(out, z[:, t, half], rhs(t), start=(t == 0), stop=(t == TB - 1))
                last.then_inc(sums_ready, 1)

            @block.scalar
            def _(act):
                for i in range(3):
                    ln_roots(nc, act, f, done=i + 1)
                for i in range(2):
                    act.wait_ge(zT_in_psum, i + 1)
                    nc.scalar.copy(zT[:, i], psT[:, i]).then_inc(zT_ready, 1)

            @block.vector
            def _(dve):
                link = chained(dve, chain)

                def affine(z, ready):
                    dve.wait_ge(f.xn_ready, TB * affine.rounds)
                    for t in range(TB):
                        last = nc.vector.tensor_tensor(z[:, t, :], f.xn[:, t, :], lng[:], ALU.mult)
                    link(last)
                    for t in range(TB):
                        last = nc.vector.tensor_tensor(z[:, t, :], z[:, t, :], lnb[:], ALU.add)
                    last.then_inc(ready, 1)
                    dve.wait_ge(ready, 1)

                dve.wait_ge(cx_loaded, 16)
                ln_stats(nc, link, f, lambda t: cx[:, t, :], LN_EPS)
                ln_apply(nc, dve, link, f, lambda t: cx[:, t, :], done=1)
                affine.rounds = 1
                affine(zk, zk_ready)
                tile = lambda t: G.X[:, b * TB + t, :]
                ln_stats(nc, link, f, tile, LN_EPS)
                ln_apply(nc, dve, link, f, tile, done=2)
                dve.wait_ge(f.xn_ready, 2 * TB)
                tile = lambda t: f.xn[:, t, :]
                ln_stats(nc, link, f, tile, LN_EPS)
                ln_apply(nc, dve, link, f, tile, done=3)
                affine.rounds = 3
                affine(zq, zq_ready)
                dve.wait_ge(sums_ready, 1)
                link(nc.vector.tensor_tensor(gsum[:], gsum[:], psG[:, :, 0:D + 2], ALU.add))

        batch_loop(nc, B, sems, body)


def cosine_weights(nc, A, G, win, gsum, coef, wwh):
    with ExitStack() as ctx:
        sb = lambda n, s, d=F32: ctx.enter_context(nc.sbuf_tensor("l1w_" + n, s, d))
        psum = lambda n, s, d=F32: ctx.enter_context(nc.psum_tensor("l1w_" + n, s, d))
        sem = ctx.enter_context(stage_semaphores(nc, "l1w_"))
        wmean, wc, u = sb("wmean", [P, KD * LH]), sb("wc", [P, KD, LW]), sb("u", [P, KD, LW])
        offdiag, corr, sq = sb("offdiag", [P, P]), sb("corr", [P, LH, LD]), sb("sq", [P, LH])
        ones = sb("ones", [P, P])
        glob = sb("glob", [P, 2 * LH])
        w1, b1, lg, lb = sb("w1", [P, 2, LD]), sb("b1", [LH, LD]), sb("lg", [LH, LD]), sb("lb", [LH, LD])
        w2, b2 = sb("w2", [LD, 3]), sb("b2", [LH, 3])
        norm, score, decorr = sb("norm", [LH, 1]), sb("score", [LH, 1]), sb("decorr", [LH, 1])
        h1, st, mv, var, std, rstd = (sb(n, s) for n, s in (("h1", [LH, LD]), ("st", [LH, 6]), ("mv", [LH, 2]),
                                                            ("var", [LH, 1]), ("std", [LH, 1]), ("rstd", [LH, 1])))
        h1T = sb("h1T", [LD, LH])
        lo, mx, ex, z, rz, w = (sb(n, s) for n, s in (("lo", [LH, 3]), ("mx", [LH, 1]), ("ex", [LH, 3]), ("z", [LH, 1]),
                                                      ("rz", [LH, 1]), ("w", [LH, 3])))
        alpha, diag = sb("alpha", [LH, 1]), sb("diag", [LH, 2 * LH])
        psU = psum("psU", [P, KD, 2, S])
        psC = psum("psC", [P, LH, LD])
        psM = psum("psM", [P, S])
        psN = psum("psN", [P, S])
        loaded, step, chain = sem("loaded"), sem("step"), sem("chain")
        to_pe, from_pe, to_act, from_act = sem("to_pe"), sem("from_pe"), sem("to_act"), sem("from_act")
        row = lambda x: x.rearrange("(a n) -> a n", a=1).partition_broadcast(LH)
        load_weights(nc, [(w1[:], A["L1_xattn_wp_w1"].rearrange("(j p) o -> p j o", p=P)), (b1[:], row(A["L1_xattn_wp_b1"])),
                          (lg[:], row(A["L1_xattn_wp_ln_g"])), (lb[:], row(A["L1_xattn_wp_ln_b"])),
                          (w2[:], A["L1_xattn_wp_w2"]), (b2[:], row(A["L1_xattn_wp_b2"]))], loaded)
        with nc.Block() as block:
            @block.tensor
            def _(pe):
                for i in range(2):
                    for h in range(LH):
                        for k in range(KD):
                            nc.tensor.matmul(psM[:, i * LH + h:i * LH + h + 1], win[:, k, h * LD:(h + 1) * LD],
                                             gsum[:, k, D + i:D + i + 1], start=(k == 0), stop=(k == KD - 1))
                pe.wait_ge(to_pe, 1)
                for m in range(KD):
                    for n in range(2):
                        for k in range(KD):
                            last = nc.tensor.matmul(psU[:, m, n, :], gsum[:, k, m * P:(m + 1) * P],
                                                    wc[:, k, n * S:(n + 1) * S], start=(k == 0), stop=(k == KD - 1))
                last.then_inc(from_pe, 1)
                pe.wait_ge(to_pe, 2)
                for h in range(LH):
                    cols = slice(h * LD, (h + 1) * LD)
                    for k in range(KD):
                        last = nc.tensor.matmul(psC[:, h, :], wc[:, k, cols], u[:, k, cols], start=(k == 0), stop=(k == KD - 1))
                last.then_inc(from_pe, 1)
                pe.wait_ge(to_pe, 3)
                nc.tensor.matmul(psN[0:LH, 0:1], sq[:], ones[:, 0:1], start=True, stop=True)
                for j in range(2):
                    last = nc.tensor.matmul(psN[0:LH, 4:4 + LD], glob[:, j * LH:(j + 1) * LH], w1[:, j, :],
                                            start=(j == 0), stop=(j == 1))
                last.then_inc(from_pe, 1)
                pe.wait_ge(to_pe, 4)
                nc.tensor.transpose(psM[:, 0:LH], h1[:], G.ident[0:LH, 0:LH]).then_inc(from_pe, 1)
                pe.wait_ge(to_pe, 5)
                nc.tensor.matmul(psN[0:LH, 0:3], h1T[:], w2[:], start=True, stop=True).then_inc(from_pe, 1)
                pe.wait_ge(to_pe, 6)
                nc.tensor.matmul(psM[:, 0:2 * LH], ones[0:LH, :], diag[:], start=True, stop=True).then_inc(from_pe, 1)

            @block.scalar
            def _(act):
                act.wait_ge(to_act, 1)
                nc.scalar.activation(score[:], norm[:], ACT.Sqrt).then_inc(from_act, 1)
                act.wait_ge(from_act, 1)
                nc.scalar.activation(decorr[:], score[:], ACT.Exp, scale=-5.0 / (LD * LD)).then_inc(from_act, 1)
                act.wait_ge(to_act, 2)
                nc.scalar.activation(std[:], var[:], ACT.Sqrt).then_inc(from_act, 1)
                act.wait_ge(to_act, 3)
                nc.scalar.activation(ex[:], lo[:], ACT.Exp).then_inc(from_act, 1)

            @block.vector
            def _(dve):
                link = chained(dve, chain)
                w3 = win[:].rearrange("p k (h d) -> p (k h) d", d=LD)
                nc.vector.memset(ones[:], 1.0)
                link(nc.vector.tensor_reduce(wmean[:], w3, AX_X, ALU.add))
                link(nc.vector.tensor_scalar(wmean[:], wmean[:], 1.0 / LD, None, ALU.mult))
                nc.vector.tensor_tensor(wc[:].rearrange("p k (h d) -> p (k h) d", d=LD), w3,
                                        wmean[:].unsqueeze(2).to_broadcast([P, KD * LH, LD]), ALU.subtract).then_inc(to_pe, 1)
                link(nc.vector.tensor_scalar(offdiag[:], G.ident[:], -1.0, 1.0, ALU.mult, ALU.add))
                dve.wait_ge(from_pe, 1)
                link(nc.vector.tensor_scalar(glob[:], psM[:, 0:2 * LH], 1.0 / N_TOK, None, ALU.mult))
                for m in range(KD):
                    last = nc.vector.tensor_copy(u[:, m, :], psU[:, m].rearrange("p n c -> p (n c)"))
                last.then_inc(to_pe, 1)
                dve.wait_ge(from_pe, 2)
                link(nc.vector.scalar_tensor_tensor(corr[:], psC[:], 1.0 / N_TOK, offdiag[:].unsqueeze(1).to_broadcast([P, LH, LD]),
                                                    ALU.mult, ALU.mult))
                link(nc.vector.tensor_tensor(corr[:], corr[:], corr[:], ALU.mult))
                nc.vector.tensor_reduce(sq[:], corr[:], AX_X, ALU.add).then_inc(to_pe, 1)
                dve.wait_ge(from_pe, 3)
                nc.vector.tensor_copy(norm[:], psN[0:LH, 0:1]).then_inc(to_act, 1)
                link(nc.vector.tensor_tensor(h1[:], psN[0:LH, 4:4 + LD], b1[:], ALU.add))
                link(nc.vector.bn_stats(st[:], h1[:]))
                link(nc.vector.bn_aggr(mv[:], st[:]))
                nc.vector.tensor_scalar(var[:], mv[:, 1:2], LN_EPS, None, ALU.add).then_inc(to_act, 1)
                dve.wait_ge(from_act, 3)
                link(nc.vector.reciprocal(rstd[:], std[:]))
                link(nc.vector.tensor_scalar(h1[:], h1[:], mv[:, 0:1], rstd[:], ALU.subtract, ALU.mult))
                link(nc.vector.tensor_tensor(h1[:], h1[:], lg[:], ALU.mult))
                link(nc.vector.tensor_tensor(h1[:], h1[:], lb[:], ALU.add))
                nc.vector.tensor_scalar(h1[:], h1[:], 0.0, None, ALU.max).then_inc(to_pe, 1)
                dve.wait_ge(from_pe, 4)
                nc.vector.tensor_copy(h1T[:], psM[:, 0:LH]).then_inc(to_pe, 1)
                dve.wait_ge(from_pe, 5)
                link(nc.vector.tensor_tensor(lo[:], psN[0:LH, 0:3], b2[:], ALU.add))
                link(nc.vector.tensor_reduce(mx[:], lo[:], AX_X, ALU.max))
                nc.vector.tensor_scalar(lo[:], lo[:], mx[:], None, ALU.subtract).then_inc(to_act, 1)
                dve.wait_ge(from_act, 4)
                link(nc.vector.tensor_reduce(z[:], ex[:], AX_X, ALU.add))
                link(nc.vector.reciprocal(rz[:], z[:]))
                link(nc.vector.tensor_scalar(w[:], ex[:], rz[:], None, ALU.mult))
                link(nc.vector.tensor_scalar(alpha[:], w[:, 1:2], decorr[:], w[:, 0:1], ALU.mult, ALU.add))
                link(nc.vector.tensor_copy(wwh[:], w[:, 2:3]))
                nc.vector.tensor_scalar(diag[:, 0:LH], G.ident[0:LH, 0:LH], alpha[:], None, ALU.mult)
                nc.vector.tensor_scalar(diag[:, LH:], G.ident[0:LH, 0:LH], w[:, 2:3], None, ALU.mult).then_inc(to_pe, 1)
                dve.wait_ge(from_pe, 6)
                link(nc.vector.tensor_copy(coef[:], psM[:, 0:2 * LH]))


def cosine_apply(nc, A, G, z_dram, win, wout, bout, coef, wwh):
    KW = LD + 1
    with ExitStack() as ctx:
        sb = lambda n, s, d=F32: ctx.enter_context(nc.sbuf_tensor("l1a_" + n, s, d))
        psum = lambda n, s, d=F32: ctx.enter_context(nc.psum_tensor("l1a_" + n, s, d))
        sem = ctx.enter_context(stage_semaphores(nc, "l1a_"))
        zT = sb("zT", [P, 2, KD, S])
        fk, kh = sb("fk", [P, TB, LW]), sb("kh", [P, TB, LH, KW])
        fq = sb("fq", [P, TB, LW])
        st = sb("st", [P, TB, LH, 6])
        mean, m2, tmp, nsq, norm, rnorm = (sb(n, [P, TB, LH]) for n in ("mean", "m2", "tmp", "nsq", "norm", "rnorm"))
        low, ratio = sb("low", [P, TB, LH]), sb("ratio", [P, TB, LH])
        kvT, rm, gs, gm = sb("kvT", [P, LH, LD]), sb("rm", [P, LH, LH]), sb("gs", [P, LH, D]), sb("gm", [LH, D])
        qT, ratioT = sb("qT", [P, LH, S]), sb("ratioT", [LH, S])
        psF, psK = psum("psF", [P, 2, S]), psum("psK", [P, 3, S])
        psG, psM = psum("psG", [P, 2, S]), psum("psM", [P, S])
        z_loaded = [sem("zk_loaded"), sem("zq_loaded")]
        f_in_psum, f_taken, nsq_ready, norm_ready, kh_ready, qh_ready = (sem(n) for n in ("f_in_psum", "f_taken", "nsq_ready", "norm_ready", "kh_ready", "qh_ready"))
        kv_in_psum, kv_ready, g_in_psum, g_taken, gm_in_psum, gm_ready = (sem(n) for n in ("kv_in_psum", "kv_ready", "g_in_psum", "g_taken", "gm_in_psum", "gm_ready"))
        q_in_psum, q_taken, ratioT_in_psum, ratioT_ready, y_ready, y_taken = (sem(n) for n in ("q_in_psum", "q_taken", "ratioT_in_psum", "ratioT_ready", "y_ready", "y_taken"))
        chain, set_up = sem("chain"), sem("set_up")
        sems = [*z_loaded, f_in_psum, f_taken, nsq_ready, norm_ready, kh_ready, qh_ready, kv_in_psum, kv_ready, g_in_psum,
                g_taken, gm_in_psum, gm_ready, q_in_psum, q_taken, ratioT_in_psum, ratioT_ready, y_ready, y_taken, chain]
        with nc.Block() as block:
            @block.vector
            def _(dve):
                nc.vector.memset(rm[:], 0.0).then_inc(set_up, 1)
                dve.wait_ge(set_up, 1)

        def kv_at(h, n):
            return psK[:, h // 3, (h % 3) * KW:(h % 3) * KW + n]

        def body(block, b):
            @block.sync
            def _(sp):
                for i in range(2):
                    sp.dma_start(zT[:, i], z_dram[i].rearrange("(k p) t -> p k t", p=P)[:, :, bass.ds(b * S, S)]
                                 ).then_inc(z_loaded[i], 16)
                for i in range(2):
                    sp.wait_ge(z_loaded[i], 16)

            @block.tensor
            def _(pe):
                def features(i):
                    pe.wait_ge(z_loaded[i], 16)
                    for t in range(TB):
                        for n in range(2):
                            if i + t > 0:
                                pe.wait_ge(f_taken, 2 * (i * TB + t - 1) + n + 1)
                            for k in range(KD):
                                last = nc.tensor.matmul(psF[:, n, :], zT[:, i, k, t * P:(t + 1) * P], win[:, k, n * S:(n + 1) * S],
                                                        start=(k == 0), stop=(k == KD - 1))
                            last.then_inc(f_in_psum, 1)

                features(0)
                features(1)
                pe.wait_ge(kh_ready, 1)
                for h in range(LH):
                    for t in range(TB):
                        last = nc.tensor.matmul(kv_at(h, KW), fk[:, t, h * LD:(h + 1) * LD], kh[:, t, h, :],
                                                start=(t == 0), stop=(t == TB - 1))
                last.then_inc(kv_in_psum, 1)
                pe.wait_ge(kv_ready, 2)
                for h in range(LH):
                    nc.tensor.matmul(psM[0:LH, 0:D], rm[:, h, :], wout[:, h, :], start=(h == 0),
                                     stop=(h == LH - 1)).then_inc(gm_in_psum, 1)
                for j in range(LH // 2):
                    if j >= 2:
                        pe.wait_ge(g_taken, 2 * (j - 1))
                    for h in (2 * j, 2 * j + 1):
                        last = nc.tensor.matmul(psG[:, j % 2, (h % 2) * D:(h % 2 + 1) * D], kvT[:, h, :], wout[:, h, :],
                                                start=True, stop=True)
                    last.then_inc(g_in_psum, 1)
                pe.wait_ge(qh_ready, 1)
                pe.wait_ge(gm_ready, 1)
                for t in range(TB):
                    last = nc.tensor.transpose(psM[0:LH, t * P:(t + 1) * P], ratio[:, t, :], G.ident[:])
                last.then_inc(ratioT_in_psum, 1)
                for h in range(LH):
                    pe.wait_ge(g_taken, LH - 2 if h == 0 else LH)
                    if h >= 2:
                        pe.wait_ge(q_taken, h - 1)
                    for t in range(TB):
                        last = nc.tensor.transpose(psG[:, h % 2, t * P:(t + 1) * P], fq[:, t, h * LD:(h + 1) * LD], G.ident[:])
                    last.then_inc(q_in_psum, 1)
                pe.wait_ge(q_taken, LH)
                pe.wait_ge(ratioT_ready, 1)
                for t in range(TB):
                    if t >= 2:
                        pe.wait_ge(y_taken, t - 1)
                    cols = slice(t * P, (t + 1) * P)
                    for h in range(LH):
                        nc.tensor.matmul(psK[:, t % 2, 0:D], qT[:, h, cols], gs[:, h, :], start=(h == 0), stop=False)
                    nc.tensor.matmul(psK[:, t % 2, 0:D], ratioT[:, cols], gm[:], start=False, stop=True).then_inc(y_ready, 1)

            @block.scalar
            def _(act):
                for i, f in enumerate((fk, fq)):
                    for t in range(TB):
                        for n in range(2):
                            act.wait_ge(f_in_psum, 2 * (i * TB + t) + n + 1)
                            nc.scalar.copy(f[:, t, n * S:(n + 1) * S], psF[:, n, :]).then_inc(f_taken, 1)
                    act.wait_ge(nsq_ready, i + 1)
                    nc.scalar.activation(norm[:], nsq[:], ACT.Sqrt).then_inc(norm_ready, 1)
                act.wait_ge(kv_in_psum, 1)
                for h in range(LH):
                    last = nc.scalar.copy(kvT[:, h, :], kv_at(h, LD))
                last.then_inc(kv_ready, 1)
                for j in range(LH // 2):
                    act.wait_ge(g_in_psum, j + 1)
                    for h in (2 * j, 2 * j + 1):
                        nc.scalar.activation(gs[:, h, :], psG[:, j % 2, (h % 2) * D:(h % 2 + 1) * D], ACT.Copy,
                                             scale=coef[:, h:h + 1]).then_inc(g_taken, 1)
                act.wait_ge(ratioT_in_psum, 1)
                nc.scalar.copy(ratioT[:], psM[0:LH, :]).then_inc(ratioT_ready, 1)
                for h in range(LH):
                    act.wait_ge(q_in_psum, h + 1)
                    nc.scalar.copy(qT[:, h, :], psG[:, h % 2, :]).then_inc(q_taken, 1)

            @block.vector
            def _(dve):
                link = chained(dve, chain)

                def norms(i, f):
                    for t in range(TB):
                        dve.wait_ge(f_taken, 2 * (i * TB + t) + 2)
                        for h in range(LH):
                            last = nc.vector.bn_stats(st[:, t, h, :], f[:, t, h * LD:(h + 1) * LD])
                    link(last)
                    link(nc.vector.tensor_tensor(tmp[:], st[:, :, :, 1], st[:, :, :, 4], ALU.subtract))
                    link(nc.vector.tensor_tensor(mean[:], st[:, :, :, 1], st[:, :, :, 4], ALU.add))
                    link(nc.vector.scalar_tensor_tensor(tmp[:], tmp[:], LD / 4.0, tmp[:], ALU.mult, ALU.mult))
                    link(nc.vector.tensor_tensor(m2[:], st[:, :, :, 2], st[:, :, :, 5], ALU.add))
                    link(nc.vector.tensor_tensor(m2[:], m2[:], tmp[:], ALU.add))
                    link(nc.vector.scalar_tensor_tensor(nsq[:], mean[:], LD / 4.0, mean[:], ALU.mult, ALU.mult))
                    nc.vector.tensor_tensor(nsq[:], nsq[:], m2[:], ALU.add).then_inc(nsq_ready, 1)
                    link(nc.vector.tensor_scalar(m2[:], m2[:], 1.0 / (LD - 1), None, ALU.mult))
                    link(nc.vector.tensor_scalar(tmp[:], m2[:], 1.0, None, ALU.add))
                    link(nc.vector.tensor_scalar(low[:], m2[:], 1.0, 2.0, ALU.min, ALU.mult))
                    link(nc.vector.reciprocal(tmp[:], tmp[:]))
                    link(nc.vector.tensor_tensor(ratio[:], low[:], tmp[:], ALU.mult))
                    dve.wait_ge(norm_ready, i + 1)
                    link(nc.vector.reciprocal(rnorm[:], norm[:]))

                norms(0, fk)
                for t in range(TB):
                    last = nc.vector.tensor_tensor(kh[:, t, :, 0:LD], fk[:, t, :].rearrange("p (h d) -> p h d", h=LH),
                                                   rnorm[:, t, :].unsqueeze(2).to_broadcast([P, LH, LD]), ALU.mult)
                nc.vector.tensor_copy(kh[:, :, :, LD], ratio[:]).then_inc(kh_ready, 1)
                dve.wait_ge(kh_ready, 1)
                norms(1, fq)
                for t in range(TB):
                    x = fq[:, t, :].rearrange("p (h d) -> p h d", h=LH)
                    last = nc.vector.tensor_tensor(x, x, rnorm[:, t, :].unsqueeze(2).to_broadcast([P, LH, LD]), ALU.mult)
                last.then_inc(qh_ready, 1)
                dve.wait_ge(kv_ready, 1)
                for h in range(LH):
                    last = nc.vector.tensor_copy(rm[:, h, h:h + 1], kv_at(h, KW)[:, LD:KW])
                last.then_inc(kv_ready, 1)
                dve.wait_ge(gm_in_psum, LH)
                nc.vector.tensor_scalar(gm[:], psM[0:LH, 0:D], wwh[:], None, ALU.mult).then_inc(gm_ready, 1)
                for t in range(TB):
                    tile = G.X[:, b * TB + t, :]
                    link(nc.vector.tensor_tensor(tile, tile, bout[:], ALU.add))
                    dve.wait_ge(y_ready, t + 1)
                    nc.vector.tensor_tensor(tile, tile, psK[:, t % 2, 0:D], ALU.add).then_inc(y_taken, 1)
                dve.wait_ge(y_taken, TB)

        batch_loop(nc, B, sems, body)



CE = 16
CAP = N_TOK // CE * 2
CF = 1024
SHF = 512
ROW = D + CE
SB = 4


def expert_choice(nc, A, G):
    assert CAP == P * SB
    rows_dram = nc.dram_tensor("l1f_rows", [N_TOK, ROW], F32).ap()
    sT_dram = nc.dram_tensor("l1f_scoresT", [CE, N_TOK], F32).ap()
    x_dram = nc.dram_tensor("l1f_x", [N_TOK, D], F32).ap()
    shared_expert(nc, A, G, rows_dram, sT_dram, x_dram)
    with ExitStack() as ctx:
        index = ctx.enter_context(nc.sbuf_tensor("l1f_index", [P, CE, SB], U32))
        choose_tokens(nc, A, G, sT_dram, index)
        run_experts(nc, A, G, rows_dram, x_dram, index)
    with ExitStack() as ctx:
        back = ctx.enter_context(stage_semaphores(nc, "l1f_"))("back")
        load_weights(nc, [(G.X[:], x_dram.rearrange("(n p) d -> p n d", p=P))], back)


def shared_expert(nc, A, G, rows_dram, sT_dram, x_dram):
    MF = SHF // P
    with ExitStack() as ctx:
        sb = lambda n, s, d=F32: ctx.enter_context(nc.sbuf_tensor("sh_" + n, s, d))
        psum = lambda n, s, d=F32: ctx.enter_context(nc.psum_tensor("sh_" + n, s, d))
        sem = ctx.enter_context(stage_semaphores(nc, "sh_"))
        f = front_buffers(nc, ctx, "sh_")
        gate, wg, wu, wd = sb("gate", [P, KD, CE]), sb("wg", [P, KD, SHF]), sb("wu", [P, KD, SHF]), sb("wd", [P, MF, D])
        score, scoreT = sb("score", [P, TB, CE]), sb("scoreT", [CE, S])
        sg, hT = sb("sg", [P, 2, S]), sb("hT", [P, MF, S])
        psT, psL = psum("psT", [P, KD, S]), psum("psL", [P, S])
        psG, psU, psY = psum("psG", [P, 1, S]), psum("psU", [P, 2, S]), psum("psY", [P, 2, S])
        loaded = sem("loaded")
        logits_ready, score_ready, scoreT_in_psum, scoreT_ready = (sem(n) for n in ("logits_ready", "score_ready", "scoreT_in_psum", "scoreT_ready"))
        gate_in_psum, up_in_psum, sg_ready, h_ready, y_ready, y_taken = (sem(n) for n in ("gate_in_psum", "up_in_psum", "sg_ready", "h_ready", "y_ready", "y_taken"))
        stored, chain = sem("stored"), sem("chain")
        sems = [*f.sems, logits_ready, score_ready, scoreT_in_psum, scoreT_ready, gate_in_psum, up_in_psum, sg_ready,
                h_ready, y_ready, y_taken, stored, chain]
        rows = lambda x: x.rearrange("(k p) d -> p k d", p=P)
        load_weights(nc, [(gate[:], rows(A["L1_ffn_gate_w"])), (wg[:], rows(A["L1_ffn_sh_gate_w"])),
                          (wu[:], rows(A["L1_ffn_sh_up_w"])), (wd[:], rows(A["L1_ffn_sh_down_w"]))], loaded)
        rows_b = rows_dram.rearrange("(b t p) d -> b p t d", p=P, t=TB)
        x_b = x_dram.rearrange("(b t p) d -> b p t d", p=P, t=TB)

        def body(block, b):
            tile = lambda t: G.X[:, b * TB + t, :]
            of_batch = lambda dram: dram[bass.ds(b, 1)].rearrange("a p t d -> p (a t) d")

            @block.sync
            def _(sp):
                sp.wait_ge(f.xn_ready, TB)
                sp.dma_start(of_batch(rows_b)[:, :, 0:D], f.xn[:]).then_inc(stored, 16)
                sp.wait_ge(score_ready, 1)
                sp.dma_start(of_batch(rows_b)[:, :, D:ROW], score[:]).then_inc(stored, 16)
                sp.wait_ge(scoreT_ready, 1)
                sp.dma_start(sT_dram[:, bass.ds(b * S, S)], scoreT[:]).then_inc(stored, 16)
                sp.wait_ge(y_taken, TB)
                sp.dma_start(of_batch(x_b), G.X[:, bass.ds(b * TB, TB), :]).then_inc(stored, 16)
                sp.wait_ge(stored, 64)

            @block.tensor
            def _(pe):
                transpose_tokens(nc, pe, f.xn, psT, G.ident, f.xn_ready, 0, f.xT_in_psum)
                pe.wait_ge(f.xT_ready, 1)
                for t in range(TB):
                    for k in range(KD):
                        last = nc.tensor.matmul(psL[:, t * CE:(t + 1) * CE], f.xT[:, k, t * P:(t + 1) * P], gate[:, k, :],
                                                start=(k == 0), stop=(k == KD - 1))
                last.then_inc(logits_ready, 1)
                for m in range(MF):
                    for w, out, done in ((wg, psG[:, 0, :], gate_in_psum), (wu, psU[:, m % 2, :], up_in_psum)):
                        if w is wg and m >= 1:
                            pe.wait_ge(sg_ready, m)
                        if w is wu and m >= 2:
                            pe.wait_ge(h_ready, m - 1)
                        for k in range(KD):
                            last = nc.tensor.matmul(out, w[:, k, m * P:(m + 1) * P], f.xT[:, k, :], start=(k == 0), stop=(k == KD - 1))
                        last.then_inc(done, 1)
                    if m == 1:
                        pe.wait_ge(score_ready, 1)
                        for t in range(TB):
                            last = nc.tensor.transpose(psL[0:CE, t * P:(t + 1) * P], score[:, t, :], G.ident[:])
                        last.then_inc(scoreT_in_psum, 1)
                pe.wait_ge(h_ready, MF)
                for t in range(TB):
                    if t >= 2:
                        pe.wait_ge(y_taken, t - 1)
                    for m in range(MF):
                        last = nc.tensor.matmul(psY[:, t % 2, 0:D], hT[:, m, t * P:(t + 1) * P], wd[:, m, :],
                                                start=(m == 0), stop=(m == MF - 1))
                    last.then_inc(y_ready, 1)

            @block.scalar
            def _(act):
                ln_roots(nc, act, f)
                act.wait_ge(f.xT_in_psum, 1)
                nc.scalar.copy(f.xT[:], psT[:]).then_inc(f.xT_ready, 1)
                act.wait_ge(logits_ready, 1)
                nc.scalar.activation(score[:], psL[:, 0:TB * CE].rearrange("p (t e) -> p t e", e=CE), ACT.Sigmoid).then_inc(score_ready, 1)
                for m in range(MF):
                    act.wait_ge(gate_in_psum, m + 1)
                    if m >= 2:
                        act.wait_ge(h_ready, m - 1)
                    nc.scalar.activation(sg[:, m % 2, :], psG[:, 0, :], ACT.Silu).then_inc(sg_ready, 1)
                act.wait_ge(scoreT_in_psum, 1)
                nc.scalar.copy(scoreT[:], psL[0:CE, :]).then_inc(scoreT_ready, 1)

            @block.vector
            def _(dve):
                link = chained(dve, chain)
                ln_stats(nc, link, f, tile, LN_EPS)
                ln_apply(nc, dve, link, f, tile)
                for m in range(MF):
                    dve.wait_ge(up_in_psum, m + 1)
                    dve.wait_ge(sg_ready, m + 1)
                    nc.vector.tensor_tensor(hT[:, m, :], psU[:, m % 2, :], sg[:, m % 2, :], ALU.mult).then_inc(h_ready, 1)
                for t in range(TB):
                    dve.wait_ge(y_ready, t + 1)
                    nc.vector.tensor_tensor(tile(t), tile(t), psY[:, t % 2, 0:D], ALU.add).then_inc(y_taken, 1)

        batch_loop(nc, B, sems, body)


def choose_tokens(nc, A, G, sT_dram, index):
    CHUNKS = P // CE
    BITS = 30
    PASS = 2
    with ExitStack() as ctx:
        sb = lambda n, s, d=F32: ctx.enter_context(nc.sbuf_tensor("ch_" + n, s, d))
        psum = lambda n, s, d=F32: ctx.enter_context(nc.psum_tensor("ch_" + n, s, d))
        sem = ctx.enter_context(stage_semaphores(nc, "ch_"))
        s128, reached = sb("s128", [P, S]), sb("reached", [P, S])
        same_i, same = sb("same_i", [P, P], I32), sb("same", [P, P])
        thr, bit, cand, keep = (sb(n, [P, 1], I32) for n in ("thr", "bit", "cand", "keep"))
        count = sb("count", [P, 1])
        s16, above, equal, rank = (sb(n, [CE, N_TOK]) for n in ("s16", "above", "equal", "rank"))
        n_above, room = sb("n_above", [CE, 1]), sb("room", [CE, 1])
        slot = sb("slot", [P, NT, CE], I32)
        slot_i = sb("slot_i", [P, NT, CE], I32)
        slot_p, slot_j = sb("slot_p", [P, NT, CE], BF16), sb("slot_j", [P, NT, CE], BF16)
        iota_i, iota_p, iota_j = sb("iota_i", [P, P], I32), sb("iota_p", [P, P], BF16), sb("iota_j", [P, SB], BF16)
        part_i, part_f = sb("part_i", [P, 1], I32), sb("part_f", [P, 1])
        tile_f = sb("tile_f", [P, NT])
        hot_p = sb("hot_p", [P, 2, CE, P], BF16)
        hot_j, numbers = sb("hot_j", [P, NT * CE, SB]), sb("numbers", [P, NT, CE, 2 * SB], BF16)
        zeros = sb("zeros", [P, P], BF16)
        token = sb("token", [P, CE, SB])
        psC, psS, psI = psum("psC", [P, S]), psum("psS", [P, NT, CE]), psum("psI", [P, CE, 2 * SB])
        loaded, iotas, set_up, chain = sem("loaded"), sem("iotas"), sem("set_up"), sem("chain")
        counted, summed = sem("counted"), sem("summed")
        slot_ready, slotT_ready, hot_ready, hot_used, index_ready = (sem(n) for n in ("slot_ready", "slotT_ready", "hot_ready", "hot_used", "index_ready"))
        with nc.Block() as block:
            @block.sync
            def _(sp):
                chunks = sT_dram.rearrange("e (c s) -> c e s", s=S)
                for c in range(CHUNKS):
                    sp.dma_start(s128[c * CE:(c + 1) * CE, :], chunks[c]).then_inc(loaded, 16)
                sp.dma_start(s16[:], sT_dram).then_inc(loaded, 16)
                sp.wait_ge(loaded, 16 * (CHUNKS + 1))

            @block.gpsimd
            def _(pool):
                nc.gpsimd.iota(same_i[:], [[-1, P]], base=P, channel_multiplier=1).then_inc(iotas, 1)
                nc.gpsimd.iota(iota_i[:], [[1, P]], base=0, channel_multiplier=0).then_inc(iotas, 1)
                nc.gpsimd.iota(part_i[:], [[0, 1]], base=0, channel_multiplier=1).then_inc(iotas, 1)
                pool.wait_ge(iotas, 3)

            @block.vector
            def _(dve):
                link = chained(dve, chain)
                nc.vector.memset(thr[:], 0)
                nc.vector.memset(zeros[:], 0.0)
                nc.vector.memset(bit[:], 1 << (BITS - 1))
                dve.wait_ge(iotas, 3)
                link(nc.vector.tensor_scalar(same_i[:], same_i[:], CE - 1, None, ALU.bitwise_and))
                link(nc.vector.tensor_scalar(same[:], same_i[:], 0.0, None, ALU.is_equal))
                nc.vector.tensor_copy(iota_p[:], iota_i[:])
                nc.vector.tensor_copy(iota_j[:], iota_i[:, 0:SB])
                nc.vector.tensor_copy(tile_f[:], iota_i[:, 0:NT])
                link(nc.vector.tensor_copy(part_f[:], part_i[:]))
        nc.sync.sem_clear(chain)
        nc.all_engine_barrier()

        def bit_body(block, i):
            @block.vector
            def _(dve):
                link = chained(dve, chain)
                for n in range(PASS):
                    link(nc.vector.tensor_tensor(cand[:], thr[:], bit[:], ALU.bitwise_or))
                    nc.vector.tensor_scalar(reached[:], s128[:], cand[:].bitcast(F32), 0.0, ALU.is_ge, ALU.add,
                                            accum_out=count[:]).then_inc(counted, 1)
                    dve.wait_ge(summed, n + 1)
                    link(nc.vector.scalar_tensor_tensor(keep[:], psC[:, 0:1], float(CAP), bit[:], ALU.is_ge, ALU.mult))
                    nc.vector.tensor_tensor(thr[:], thr[:], keep[:], ALU.bitwise_or)
                    link(nc.vector.tensor_scalar(bit[:], bit[:], 1, None, ALU.logical_shift_right))

            @block.tensor
            def _(pe):
                for n in range(PASS):
                    pe.wait_ge(counted, n + 1)
                    nc.tensor.matmul(psC[:, 0:1], same[:], count[:], start=True, stop=True).then_inc(summed, 1)

        batch_loop(nc, BITS // PASS, [chain, counted, summed], bit_body)

        with nc.Block() as block:
            @block.vector
            def _(dve):
                link = chained(dve, chain)
                t = thr[0:CE, :].bitcast(F32)
                link(nc.vector.tensor_scalar(above[:], s16[:], t, 0.0, ALU.is_gt, ALU.add, accum_out=n_above[:]))
                nc.vector.tensor_scalar(room[:], n_above[:], -1.0, float(CAP), ALU.mult, ALU.add)
                link(nc.vector.tensor_scalar(equal[:], s16[:], t, None, ALU.is_equal))
                link(nc.vector.tensor_tensor_scan(rank[:], equal[:], equal[:], 0.0, ALU.add, ALU.max))
                link(nc.vector.scalar_tensor_tensor(equal[:], rank[:], room[:], equal[:], ALU.is_le, ALU.mult))
                link(nc.vector.tensor_tensor(above[:], above[:], equal[:], ALU.add))
                link(nc.vector.tensor_tensor_scan(rank[:], above[:], above[:], 0.0, ALU.add, ALU.max))
                link(nc.vector.scalar_tensor_tensor(rank[:], rank[:], 2.0 * CAP, above[:], ALU.subtract, ALU.mult))
                nc.vector.tensor_scalar(rank[:], rank[:], 2.0 * CAP - 1.0, None, ALU.add).then_inc(slot_ready, 1)
                dve.wait_ge(slotT_ready, 1)
                link(nc.vector.tensor_copy(slot_i[:], psS[:]))
                link(nc.vector.tensor_scalar(slot[:], slot_i[:], 2, None, ALU.logical_shift_right))
                nc.vector.tensor_copy(slot_p[:], slot[:])
                link(nc.vector.tensor_scalar(slot_i[:], slot_i[:], SB - 1, None, ALU.bitwise_and))
                link(nc.vector.tensor_copy(slot_j[:], slot_i[:]))
                link(nc.vector.tensor_tensor(hot_j[:], slot_j[:].rearrange("p n e -> p (n e)").unsqueeze(2).to_broadcast([P, NT * CE, SB]),
                                             iota_j[:].unsqueeze(1).to_broadcast([P, NT * CE, SB]), ALU.is_equal))
                hot = hot_j[:].rearrange("p (n e) j -> p n e j", e=CE)
                nc.vector.tensor_scalar(numbers[:, :, :, 0:SB], hot, part_f[:], None, ALU.mult)
                link(nc.vector.tensor_tensor(numbers[:, :, :, SB:], hot,
                                             tile_f[:].unsqueeze(2).unsqueeze(3).to_broadcast([P, NT, CE, SB]), ALU.mult))

            @block.tensor
            def _(pe):
                nc.tensor.matmul(psI[:].rearrange("p e j -> p (e j)"), zeros[:], zeros[:], start=True, stop=True)
                pe.wait_ge(slot_ready, 1)
                for c in range(NT):
                    last = nc.tensor.transpose(psS[:, c, :], rank[:, c * P:(c + 1) * P], G.ident[0:CE, 0:CE])
                last.then_inc(slotT_ready, 1)
        nc.sync.sem_clear(chain)
        nc.all_engine_barrier()

        ROUND = 4

        def place_body(block, i):
            @block.vector
            def _(dve):
                for n in range(ROUND):
                    if n >= 2:
                        dve.wait_ge(hot_used, n - 1)
                    where = slot_p[:, bass.ds(i * ROUND + n, 1), :].rearrange("p a e -> p (a e)").unsqueeze(2).to_broadcast([P, CE, P])
                    nc.vector.tensor_tensor(hot_p[:, n % 2], where, iota_p[:].unsqueeze(1).to_broadcast([P, CE, P]),
                                            ALU.is_equal).then_inc(hot_ready, 1)

            @block.tensor
            def _(pe):
                for n in range(ROUND):
                    pe.wait_ge(hot_ready, n + 1)
                    for e in range(CE):
                        last = nc.tensor.matmul(psI[:, e, :], hot_p[:, n % 2, e, :], numbers[:, i * ROUND + n, e, :],
                                                start=False, stop=False, skip_group_check=True)
                    last.then_inc(hot_used, 1)

        batch_loop(nc, NT // ROUND, [hot_ready, hot_used], place_body)

        with nc.Block() as block:
            @block.vector
            def _(dve):
                nc.vector.tensor_scalar(token[:], psI[:, :, SB:], float(P), None, ALU.mult).then_inc(index_ready, 1)
                dve.wait_ge(index_ready, 1)
                nc.vector.tensor_tensor(index[:], token[:], psI[:, :, 0:SB], ALU.add).then_inc(index_ready, 1)
                dve.wait_ge(index_ready, 2)


def run_experts(nc, A, G, rows_dram, x_dram, index):
    MF = CF // P
    PAIR = 2
    with ExitStack() as ctx:
        sb = lambda n, s, d=F32: ctx.enter_context(nc.sbuf_tensor("ex_" + n, s, d))
        psum = lambda n, s, d=F32: ctx.enter_context(nc.psum_tensor("ex_" + n, s, d))
        sem = ctx.enter_context(stage_semaphores(nc, "ex_"))
        wu, wg = sb("wu", [P, PAIR, KD, CF]), sb("wg", [P, PAIR, KD, CF])
        wd = sb("wd", [P, PAIR, MF, D])
        ub, gb, db = sb("ub", [P, CE, MF]), sb("gb", [P, CE, MF]), sb("db", [P, CE, D])
        idx = sb("idx", [P, PAIR, SB], U32)
        xg, xgT = sb("xg", [P, PAIR, SB, ROW]), sb("xgT", [P, KD, CAP])
        weight = sb("weight", [P, SB])
        sg, hT = sb("sg", [P, 2, CAP]), sb("hT", [P, MF, CAP])
        y = sb("y", [P, SB, D])
        psT = psum("psT", [P, KD, CAP])
        psU, psG, psY = psum("psU", [P, 2, CAP]), psum("psG", [P, 2, CAP]), psum("psY", [P, 2, S])
        loaded = sem("loaded")
        w_loaded = [sem("w0_loaded"), sem("w1_loaded")]
        gathered, added = G.gathered, G.added
        idx_ready, xT_in_psum, xT_ready, gate_in_psum, up_in_psum, sg_ready, h_ready, y_ready, y_taken, y_scaled, down_done, chain = (
            sem(n) for n in ("idx_ready", "xT_in_psum", "xT_ready", "gate_in_psum", "up_in_psum", "sg_ready", "h_ready",
                             "y_ready", "y_taken", "y_scaled", "down_done", "chain"))
        sems = [*w_loaded, idx_ready, xT_in_psum, xT_ready, gate_in_psum, up_in_psum, sg_ready, h_ready,
                y_ready, y_taken, y_scaled, down_done, chain]
        db_src = A["L1_ffn_down_b"].rearrange("e d -> (e d)").rearrange("(a n) -> a n", a=1).partition_broadcast(P)
        load_weights(nc, [(ub[:], A["L1_ffn_up_b"]), (gb[:], A["L1_ffn_gb"]),
                          (db[:].rearrange("p e d -> p (e d)"), db_src)], loaded)

        def load_expert(sp, s, e):
            one = lambda x, p_: x[bass.ds(e, 1)].rearrange("a (k p) f -> p (a k) f", p=P)
            for tile, src in ((wu, "L1_ffn_up_w"), (wg, "L1_ffn_gw"), (wd, "L1_ffn_down_w")):
                sp.dma_start(tile[:, s], one(A[src], P)).then_inc(w_loaded[s], 16)

        with nc.Block() as block:
            @block.sync
            def _(sp):
                load_expert(sp, 0, 0)
                sp.wait_ge(w_loaded[0], 48)
        nc.sync.sem_clear(w_loaded[0])
        nc.all_engine_barrier()

        GATHERED, ADDED = 16 * SB, 16 * SB * PAIR

        def body(block, i):
            @block.sync
            def _(sp):
                load_expert(sp, 1, i * PAIR + 1)
                sp.wait_ge(down_done, 1)
                load_expert(sp, 0, (i * PAIR + 2) % CE)
                for s in range(PAIR):
                    sp.wait_ge(w_loaded[s], 48)

            @block.gpsimd
            def _(pool):
                pool.wait_ge(idx_ready, 1)
                for s in range(PAIR):
                    for j in range(SB):
                        nc.gpsimd.indirect_dma_start(out=xg[:, s, j, :], out_offset=None, in_=rows_dram,
                                                     in_offset=bass.IndirectOffsetOnAxis(idx[:, s, j:j + 1], 0)).then_inc(gathered[s], 16)
                for s in range(PAIR):
                    for j in range(SB):
                        pool.wait_ge(y_scaled, s * SB + j + 1)
                        nc.gpsimd.indirect_dma_start(out=x_dram, out_offset=bass.IndirectOffsetOnAxis(idx[:, s, j:j + 1], 0),
                                                     in_=y[:, j, :], in_offset=None, compute_op=ALU.add).then_inc(added, 16)
                pool.wait_ge(added, i * ADDED + ADDED)

            @block.tensor
            def _(pe):
                for s in range(PAIR):
                    pe.wait_ge(gathered[s], i * GATHERED + GATHERED)
                    if s > 0:
                        pe.wait_ge(xT_ready, s)
                    for j in range(SB):
                        for k in range(KD):
                            last = nc.tensor.transpose(psT[:, k, j * P:(j + 1) * P], xg[:, s, j, k * P:(k + 1) * P], G.ident[:])
                    last.then_inc(xT_in_psum, 1)
                    pe.wait_ge(xT_ready, s + 1)
                    if s > 0:
                        pe.wait_ge(w_loaded[s], 48)
                    for m in range(MF):
                        n = s * MF + m
                        if n >= 2:
                            pe.wait_ge(sg_ready, n - 1)
                            pe.wait_ge(h_ready, n - 1)
                        for w, out, done in ((wg, psG, gate_in_psum), (wu, psU, up_in_psum)):
                            for k in range(KD):
                                last = nc.tensor.matmul(out[:, n % 2, :], w[:, s, k, m * P:(m + 1) * P], xgT[:, k, :],
                                                        start=(k == 0), stop=(k == KD - 1))
                            last.then_inc(done, 1)
                    pe.wait_ge(h_ready, (s + 1) * MF)
                    for j in range(SB):
                        n = s * SB + j
                        if n >= 2:
                            pe.wait_ge(y_taken, n - 1)
                        for m in range(MF):
                            last = nc.tensor.matmul(psY[:, n % 2, 0:D], hT[:, m, j * P:(j + 1) * P], wd[:, s, m, :],
                                                    start=(m == 0), stop=(m == MF - 1))
                        last.then_inc(y_ready, 1)

            @block.scalar
            def _(act):
                for s in range(PAIR):
                    e = i * PAIR + s
                    act.wait_ge(xT_in_psum, s + 1)
                    if s > 0:
                        act.wait_ge(up_in_psum, s * MF)
                    nc.scalar.copy(xgT[:], psT[:]).then_inc(xT_ready, 1)
                    for m in range(MF):
                        n = s * MF + m
                        act.wait_ge(gate_in_psum, n + 1)
                        if n >= 2:
                            act.wait_ge(h_ready, n - 1)
                        nc.scalar.activation(sg[:, n % 2, :], psG[:, n % 2, :], ACT.Silu, bias=gb[:, e, m:m + 1], scale=1.0).then_inc(sg_ready, 1)

            @block.vector
            def _(dve):
                link = chained(dve, chain)
                nc.vector.tensor_copy(idx[:], index[:, bass.ds(i * PAIR, PAIR), :]).then_inc(idx_ready, 1)
                for s in range(PAIR):
                    e = i * PAIR + s
                    dve.wait_ge(gathered[s], i * GATHERED + GATHERED)
                    for m in range(MF):
                        n = s * MF + m
                        dve.wait_ge(sg_ready, n + 1)
                        dve.wait_ge(up_in_psum, n + 1)
                        if s > 0 and m == 0:
                            dve.wait_ge(y_ready, s * SB)
                        nc.vector.scalar_tensor_tensor(hT[:, m, :], psU[:, n % 2, :], ub[:, e, m:m + 1], sg[:, n % 2, :],
                                                       ALU.add, ALU.mult).then_inc(h_ready, 1)
                    link(nc.vector.tensor_copy(weight[:], xg[:, s, :, bass.ds(e + D, 1)].rearrange("p j a -> p (j a)")))
                    if s > 0:
                        dve.wait_ge(added, i * ADDED + 16 * SB * s)
                    for j in range(SB):
                        n = s * SB + j
                        dve.wait_ge(y_ready, n + 1)
                        nc.vector.tensor_tensor(y[:, j, :], psY[:, n % 2, 0:D], db[:, e, :], ALU.add).then_inc(y_taken, 1)
                        dve.wait_ge(y_taken, n + 1)
                        nc.vector.tensor_scalar(y[:, j, :], y[:, j, :], weight[:, j:j + 1], None, ALU.mult).then_inc(y_scaled, 1)
                    if s == 0:
                        dve.sem_inc(down_done, 1)

        batch_loop(nc, CE // PAIR, sems, body)



def build_program(nc, A, out, stages):
    with ExitStack() as ctx:
        sb = lambda n, s, d=F32: ctx.enter_context(nc.sbuf_tensor(n, s, d))
        sem = lambda n: ctx.enter_context(nc.semaphore(n))
        G = Shared()
        G.X = sb("X", [P, NT, D])
        G.ident = sb("ident", [P, P])
        G.identb = sb("identb", [P, P], BF16)
        G.gathered, G.added = [sem("gathered0"), sem("gathered1")], sem("added")
        x_loaded, ident_set, stored = sem("x_loaded"), sem("ident_set"), sem("stored")
        x_dram = A["x"].rearrange("b s d -> (b s) d").rearrange("(n p) d -> p n d", p=P)
        out_dram = out.rearrange("b s d -> (b s) d").rearrange("(n p) d -> p n d", p=P)
        with nc.Block() as block:
            @block.sync
            def _(sp):
                sp.dma_start(G.X[:], x_dram).then_inc(x_loaded, 16)
                sp.wait_ge(x_loaded, 16)

            @block.gpsimd
            def _(pool):
                nc.gpsimd.memset(G.ident[:], 0.0).then_inc(ident_set, 1)
                pool.wait_ge(ident_set, 1)
                nc.gpsimd.affine_select(out=G.ident[:], in_=G.ident[:], compare_op=ALU.not_equal, fill=1.0, base=0,
                                        pattern=[[-1, P]], channel_multiplier=1).then_inc(ident_set, 1)
                pool.wait_ge(ident_set, 2)
                nc.gpsimd.tensor_copy(G.identb[:], G.ident[:]).then_inc(ident_set, 1)
                pool.wait_ge(ident_set, 3)

        for stage in stages:
            STAGES[stage](nc, A, G)

        with nc.Block() as block:
            @block.sync
            def _(sp):
                sp.dma_start(out_dram, G.X[:]).then_inc(stored, 16)
                sp.wait_ge(stored, 16)


STAGES = {"attn0": attention0, "ffn0": moe_top1, "attn1": cosine_attention, "ffn1": expert_choice, "attn2": attention2, "ffn2": pwl_ffn, "attn3": attention3,
          "ffn3": moe_top2}
ORDER = ["attn0", "ffn0", "attn1", "ffn1", "attn2", "ffn2", "attn3", "ffn3"]




def host_layout(inputs):
    import numpy as np

    a = {k: np.asarray(v) for k, v in inputs.items()}
    for name in ["L0_xattn_Wv", "L0_xattn_Wk", "L0_xattn_Wq", "L0_xattn_Wo", "L1_xattn_w_in", "L1_xattn_wp_w1",
                 "L1_xattn_wp_w2", "L1_xattn_w_out", "L1_ffn_gate_w", "L1_ffn_sh_gate_w", "L1_ffn_sh_up_w",
                 "L1_ffn_sh_down_w", "L2_xattn_Wq", "L2_xattn_Wk", "L2_xattn_Wv", "L2_xattn_Wo"]:
        a[name] = a[name].T
    for name in ["L1_ffn_up_w", "L1_ffn_gw", "L1_ffn_down_w"]:
        a[name] = a[name].transpose(0, 2, 1)
    for name in ["L2_ffn_b1", "L0_xattn_bq", "L0_xattn_bk", "L2_xattn_bq", "L2_xattn_bk", "L3_xattn_bq"]:
        a[name] = a[name].reshape(-1, P).T
    a["L3_xattn_bk"] = a["L3_xattn_bkv"][:D].reshape(-1, P).T
    a["L1_ffn_up_b"] = a["L1_ffn_up_b"].reshape(16, -1, P).transpose(2, 0, 1)
    a["L1_ffn_gb"] = a["L1_ffn_gb"].reshape(16, -1, P).transpose(2, 0, 1)
    a["ctxT"] = a["ctx_1024"].reshape(N_TOK, D).T
    a["maskT"] = a["mask_Bx1xSxS2_ik1"][:, 0].transpose(0, 2, 1)
    return {k: np.ascontiguousarray(v) for k, v in a.items()}


def kernel(**inputs):
    import numpy as np
    import concourse.bacc as bacc
    from concourse.bass_utils import run_bass_kernel_spmd

    nc = bacc.Bacc("TRN2", target_bir_lowering=False, num_devices=1)
    arrays = host_layout(inputs)
    A = {n: nc.dram_tensor(f"in_{n}", list(a.shape), mybir.dt.from_np(a.dtype), kind="ExternalInput").ap()
         for n, a in arrays.items()}
    out = nc.dram_tensor("out", [B, S, D], F32, kind="ExternalOutput").ap()
    build_program(nc, A, out, ORDER)
    r = run_bass_kernel_spmd(nc, [{f"in_{n}": a for n, a in arrays.items()}], core_ids=[0])
    return r.results[0]["out"]
```
